# Optimizing a Trainium2 kernel written in Bass

```python
import numpy as np
import jax
import jax.numpy as jnp

def _softmax(x, axis=-1):
    return jax.nn.softmax(x, axis=axis)

def _gelu(x):
    return jax.nn.gelu(x, approximate=True)

def _silu(x):
    return jax.nn.silu(x)

def _sigmoid(x):
    return jax.nn.sigmoid(x)

def _layernorm(x, axis=-1, eps=1e-05):
    m = jnp.mean(x, axis=axis, keepdims=True)
    v = jnp.var(x, axis=axis, keepdims=True)
    return (x - m) / jnp.sqrt(v + eps)

def _scatter_add(tgt, idx, src, axis=0):
    return tgt.at[idx].add(src)

def _segment_sum(src, seg, n):
    return jax.ops.segment_sum(src, seg, n)
kernel_name = 'mk_prb_d1_jaxref_r8_327a07'

def setup_inputs(seed: int=0):
    np.random.seed(seed)
    _w = jnp.asarray

    def _L0_attn_setup():
        import jax, jax.numpy as jnp
        import numpy as np
        D = 128
        K_LOW1 = D // 4
        K_LOW2 = D // 4

        def mix_precision_matmul(x, w):
            d = x.shape[-1]
            w1 = w[:K_LOW1]
            wh = w[K_LOW1:d - K_LOW2]
            w2 = w[d - K_LOW2:]
            y1 = jnp.matmul(x[..., :K_LOW1].astype(jnp.float16), w1.astype(jnp.float16)).astype(jnp.float32)
            yh = jnp.matmul(x[..., K_LOW1:d - K_LOW2], wh)
            y2 = jnp.matmul(x[..., d - K_LOW2:].astype(jnp.float16), w2.astype(jnp.float16)).astype(jnp.float32)
            return y1 + yh + y2
        key = jax.random.key(seed)
        k1, k2, k3, k4 = jax.random.split(key, 4)
        B, N, d = (8, 256, D)
        x = jax.random.normal(k1, (B, N, d), dtype=jnp.float32)
        weight_qkv = jax.random.normal(k2, (d, 3 * d), dtype=jnp.float32) * d ** (-0.5)
        out_w = jax.random.normal(k3, (d, d), dtype=jnp.float32) * d ** (-0.5)
        out_b = jax.random.normal(k4, (d,), dtype=jnp.float32) * 0.01
        return {'x': x, 'weight_qkv': weight_qkv, 'out_w': out_w, 'out_b': out_b}
    _L0_attn_in = _L0_attn_setup()

    def _L0_ffn_setup():
        import jax, jax.numpy as jnp
        import numpy as np
        B, T = (2, 256)
        D_MODEL, D_HIDDEN = (128, 256)
        N_EXPERTS, TOP_K = (8, 2)
        N_TOKENS = B * T
        CAPACITY = 2 * N_TOKENS * TOP_K // N_EXPERTS
        key = jax.random.key(seed)
        k_x, k_rw, k_w, k_v, k_o = jax.random.split(key, 5)
        x = jax.random.normal(k_x, (B, T, D_MODEL), jnp.float32)
        router_w = jax.random.normal(k_rw, (N_EXPERTS, D_MODEL), jnp.float32) * D_MODEL ** (-0.5)
        router_b = jnp.zeros((N_EXPERTS,), jnp.float32)
        W = jax.random.normal(k_w, (N_EXPERTS, D_MODEL, D_HIDDEN), jnp.float32) * D_MODEL ** (-0.5)
        V = jax.random.normal(k_v, (N_EXPERTS, D_MODEL, D_HIDDEN), jnp.float32) * D_MODEL ** (-0.5)
        W_out = jax.random.normal(k_o, (N_EXPERTS, D_HIDDEN, D_MODEL), jnp.float32) * D_HIDDEN ** (-0.5)
        return {'x': x, 'router_w': router_w, 'router_b': router_b, 'W': W, 'V': V, 'W_out': W_out}
    _L0_ffn_in = _L0_ffn_setup()
    _d = {'L0_attn_x': _L0_attn_in['x'], 'L0_attn_weight_qkv': _L0_attn_in['weight_qkv'], 'L0_attn_out_w': _L0_attn_in['out_w'], 'L0_attn_out_b': _L0_attn_in['out_b'], 'L0_ffn_router_w': _L0_ffn_in['router_w'], 'L0_ffn_router_b': _L0_ffn_in['router_b'], 'L0_ffn_W': _L0_ffn_in['W'], 'L0_ffn_V': _L0_ffn_in['V'], 'L0_ffn_W_out': _L0_ffn_in['W_out']}
    _x0 = _d['L0_attn_x']
    _d['L0_attn_x'] = jax.random.normal(jax.random.fold_in(jax.random.key(seed), 1), (4, 1024, 128), dtype=_x0.dtype)
    del _x0
    return _d

def reference(L0_attn_x, L0_attn_weight_qkv, L0_attn_out_w, L0_attn_out_b, L0_ffn_router_w, L0_ffn_router_b, L0_ffn_W, L0_ffn_V, L0_ffn_W_out):

    def _L0_attn_ref(x, weight_qkv, out_w, out_b):
        import jax, jax.numpy as jnp
        import numpy as np
        D = 128
        K_LOW1 = D // 4
        K_LOW2 = D // 4

        def mix_precision_matmul(x, w):
            d = x.shape[-1]
            w1 = w[:K_LOW1]
            wh = w[K_LOW1:d - K_LOW2]
            w2 = w[d - K_LOW2:]
            y1 = jnp.matmul(x[..., :K_LOW1].astype(jnp.float16), w1.astype(jnp.float16)).astype(jnp.float32)
            yh = jnp.matmul(x[..., K_LOW1:d - K_LOW2], wh)
            y2 = jnp.matmul(x[..., d - K_LOW2:].astype(jnp.float16), w2.astype(jnp.float16)).astype(jnp.float32)
            return y1 + yh + y2
        d = x.shape[-1]
        qkv = mix_precision_matmul(x, weight_qkv)
        q, k, v = jnp.split(qkv, 3, axis=-1)
        q = q / jnp.sqrt(jnp.asarray(d, dtype=q.dtype))
        qk = jnp.einsum('bqd,bkd->bqk', q, k)
        s = jax.nn.softmax(qk, axis=-1)
        y = jnp.einsum('bqk,bkd->bqd', s, v)
        return jnp.matmul(y, out_w.T) + out_b

    def _L0_ffn_ref(x, router_w, router_b, W, V, W_out):
        import jax, jax.numpy as jnp
        import numpy as np
        B, T = (2, 256)
        D_MODEL, D_HIDDEN = (128, 256)
        N_EXPERTS, TOP_K = (8, 2)
        N_TOKENS = B * T
        CAPACITY = 2 * N_TOKENS * TOP_K // N_EXPERTS
        Bq, Tq, D = x.shape
        N = Bq * Tq
        x_flat = x.reshape(N, D)
        router_logits = x_flat @ router_w.T + router_b
        top_vals, top_ids = jax.lax.top_k(router_logits, TOP_K)
        top_probs = jax.nn.softmax(top_vals, axis=-1)
        x_pad = jnp.concatenate([x_flat, jnp.zeros((1, D), x_flat.dtype)], axis=0)
        probs_pad = jnp.concatenate([top_probs, jnp.zeros((1, TOP_K), top_probs.dtype)], axis=0)
        out = jnp.zeros((N + 1, D), x_flat.dtype)
        for e in range(N_EXPERTS):
            tok, slot = jnp.nonzero(top_ids == e, size=CAPACITY, fill_value=(N, 0))
            w = probs_pad[tok, slot][:, None]
            xin = x_pad[tok]
            a = xin @ W[e]
            b = xin @ V[e]
            y = a * (b * jax.nn.sigmoid(b)) @ W_out[e]
            out = out.at[tok].add(y * w)
        return out[:N].reshape(Bq, Tq, D)
    x = L0_attn_x
    xn = _layernorm(x, axis=-1)
    x = x + _L0_attn_ref(xn, L0_attn_weight_qkv, L0_attn_out_w, L0_attn_out_b) + _L0_ffn_ref(xn, L0_ffn_router_w, L0_ffn_router_b, L0_ffn_W, L0_ffn_V, L0_ffn_W_out)
    return x

_drawn_inputs = setup_inputs


def setup_inputs(seed=0):
    import zlib

    import numpy as np

    out = dict(_drawn_inputs(seed))
    spreads = {'L0_ffn_router_b': (0.0, 0.1)}
    factors = {'L0_attn_out_b': 5.679}
    for name, (base, spread) in spreads.items():
        noise = np.random.default_rng([zlib.crc32(name.encode()), seed]).standard_normal(out[name].shape)
        drawn = base * np.exp(spread * noise) if base else spread * noise
        out[name] = jnp.asarray(drawn.astype(out[name].dtype))
    for name, factor in factors.items():
        out[name] = (out[name] * factor).astype(out[name].dtype)
    return out
```

```python
from contextlib import ExitStack

import concourse.bass as bass
from concourse import mybir

F32 = mybir.dt.float32
F16 = mybir.dt.float16
I32 = mybir.dt.int32
ALU = mybir.AluOpType
ACT = mybir.ActivationFunctionType
AX = mybir.AxisListType.X

P = 128
EPS = 1e-5
HI, LO = 0, 1
W_SCALE = 64.0
BIG = 3.0e38
STEPS = 4


def block_kernel(nc, x, w_qkv, out_wT, out_b, router_wT, router_b, w_in, v_in, w_out, out):
    B, T, D = x.shape
    N = B * T
    NT = N // P
    BT = T // P
    E, _, H = w_in.shape
    HB = H // P
    CAP = 2 * 512 * 2 // E
    CB = CAP // P
    NS = E * CB
    LOW = D // 4
    G = 4
    NG = NT // G
    ITS = NT // STEPS
    GC = G * P
    RC = 2 * P + 2
    assert D == P and HB == 2 and CB == 2 and BT == 8 and B == 4

    Q_EVAC = 4.0 / (float(D) ** 0.5 * W_SCALE)
    K_EVAC = 1.0 / (4.0 * W_SCALE)
    V_EVAC = 1.0 / W_SCALE

    xg_dram = nc.dram_tensor("xn_hi_lo", (N, 2 * D), F16, kind="Internal").ap()
    sum_dram = nc.dram_tensor("x_bias_experts", (N + CAP, D), F32, kind="Internal").ap()

    with ExitStack() as ctx:
        def sb(name, shape, dt=F32):
            return ctx.enter_context(nc.sbuf_tensor(name, shape, dt))

        def psum(name, shape):
            return ctx.enter_context(nc.psum_tensor(name, shape, F32))

        def sem(name):
            return ctx.enter_context(nc.semaphore(name))

        psS = psum("psS", [P, 2, 2, 512])
        psT = psum("psT", [P, 2, 512])
        psO = psum("psO", [P, 512])
        psM = psum("psM", [P, 512])

        x_sb = sb("x_sb", [P, NT, D])
        probs = sb("probs", [P, 2, T])
        xhl = sb("xhl", [P, NT, 2 * D], F16)
        xT = sb("xT", [P, 2, N], F16)
        qT = sb("qT", [P, 2, N], F16)
        kT = sb("kT", [P, 2, N], F16)
        vp = sb("vp", [P, NT, 2, D], F16)
        attn = sb("attn", [P, NT, D])
        vT = attn[:].rearrange("p n d -> p (n d)").bitcast(F16).rearrange("p (s n) -> p s n", s=2)
        shared = sb("shared", [P, 4096])
        wv_in = shared[:].rearrange("p (e h) -> p e h", e=E)
        half = NS * D
        xg = shared[:, 0:half].bitcast(F16).rearrange("p (s c) -> p s c", s=NS)
        y_sb = shared[:, half:2 * half].rearrange("p (s d) -> p s d", s=NS)
        wv = sb("wv", [P, 2, E, 2 * H], F16)
        wo_in = sb("wo_in", [P, E, HB * D])
        wo = sb("wo", [P, 2, E, HB * D], F16)
        pT = sb("pT", [P, 2, 2, T], F16)
        qkv_in = sb("qkv_in", [P, 3 * D])
        w_all = sb("w_all", [P, 3 * D], F16)
        w_mid = sb("w_mid", [P, 2, 3 * D], F16)
        owT_in = sb("owT_in", [P, D])
        owT = sb("owT", [P, 2, D], F16)
        rw_in = sb("rw_in", [P, E])
        rw = sb("rw", [P, 2, E], F16)
        rb = sb("rb", [P, E])
        bias = sb("bias", [P, D])

        ident = sb("ident", [P, P])
        ident16 = sb("ident16", [P, P], F16)
        upper = sb("upper", [P, P], F16)
        below = sb("below", [NT, NT], F16)
        slot_i = sb("slot_i", [P, CAP], I32)
        slot_row = sb("slot_row", [NT, CAP], F16)
        slot_col_i = sb("slot_col_i", [P, NS], I32)
        slot_col = sb("slot_col", [P, NS])
        slot_next = sb("slot_next", [P, NS])
        slot_dump = sb("slot_dump", [P, NS])
        rank_i = sb("rank_i", [P, E], I32)
        rank = sb("rank", [P, E])
        tile_i = sb("tile_i", [NT, 2], I32)

        stats = sb("stats", [P, NT, 6])
        mv = sb("mv", [P, NT, 2])
        std = sb("std", [P, NT])
        rstd = sb("rstd", [P, NT])

        logits, rest, first, second = (probs[:, 1, k * NT * E:(k + 1) * NT * E].rearrange("p (n e) -> p n e", e=E)
                                       for k in range(4))
        ta = sb("ta", [P, NT, E])
        top1 = sb("top1", [P, NT])
        top2 = sb("top2", [P, NT])
        pick = sb("pick", [P, NT])
        gap = sb("gap", [P, NT])
        egap = sb("egap", [P, NT])
        gate1 = sb("gate1", [P, NT])
        gate2 = sb("gate2", [P, NT])
        mask = sb("mask", [P, NT, E], F16)
        tot = sb("tot", [NT, E], F16)
        start = sb("start", [NT, E])
        end = sb("end", [NT, E])
        before_end = probs[0:NT, 0, :].bitcast(F16).rearrange("p (e c) -> p e c", e=E)
        in_tile = sb("in_tile", [NT, E, CAP], F16)
        row_src = sb("row_src", [NT, E, RC], F16)
        row_lo = sb("row_lo", [NT, E, P], F16)
        row = sb("row", [P, 4, RC])
        count = sb("count", [P, NS])
        aux = sb("aux", [P, NS, 2])
        slot_w = sb("slot_w", [P, NS])
        slot_ws = sb("slot_ws", [P, NS])
        unused = sb("unused", [P, NS])
        where = sb("where", [P, NS])
        to_row = sb("to_row", [P, NS], I32)
        from_row = sb("from_row", [P, NS], I32)

        neg_max = sb("neg_max", [P, 4])
        row_sum = sb("row_sum", [P, 4])
        inv_sum = sb("inv_sum", [P, 4])

        xT_flat = xT[:].rearrange("p s n -> p (s n)")
        assert 14 * HB * CAP <= 2 * N

        def after_xT(k, size, dt=F16):
            return xT_flat[:, k * HB * CAP:k * HB * CAP + size].bitcast(dt) if dt != F16 else \
                xT_flat[:, k * HB * CAP:k * HB * CAP + size]

        HC = HB * CAP
        xgT = after_xT(0, 4 * CAP).rearrange("p (q s c) -> p q s c", q=2, s=2)
        hidT = after_xT(2, 4 * HC).rearrange("p (q s c) -> p q s c", q=2, s=2)
        hid = after_xT(6, 4 * HC, F32).rearrange("p (q c) -> p q c", q=2)
        silu = after_xT(10, 2 * HC, F32)
        tanh_b = after_xT(12, 2 * HC, F32)

        x_in = [sem(f"x_in{b}") for b in range(B)]
        small_in, w_in_s, wo_in_s = sem("small_in"), sem("w_in"), sem("wo_in")
        zeroed, consts_i, consts = sem("zeroed"), sem("consts_i"), sem("consts")
        stat_s, var_s, std_s, rstd_s, xn_s = sem("stat"), sem("var"), sem("std"), sem("rstd"), sem("xn")
        x_hi, x_lo = sem("x_hi"), sem("x_lo")
        xb_s, xb_out, xg_out = sem("xb"), sem("xb_out"), sem("xg_out")
        small_w = sem("small_w")
        wv_hi, wv_lo, wo_hi, wo_lo, w_up = sem("wv_hi"), sem("wv_lo"), sem("wo_hi"), sem("wo_lo"), sem("w_up")
        xT_ps, xT_s = sem("xT_ps"), sem("xT")
        scores_r = sem("router_scores")
        route = sem("route")
        gap_s, egap_s, plan_in = sem("gap"), sem("egap"), sem("plan_in")
        counts_ps, gates_ps, start_ps = sem("counts_ps"), sem("gates_ps"), sem("start_ps")
        row_hi, row_lo_s, tot_s, plan_s = sem("row_hi"), sem("row_lo"), sem("tot"), sem("plan")
        unit_ps, unit_hi, unit_lo = sem("unit_ps"), sem("unit_hi"), sem("unit_lo")
        s_ready, max_done, exp_done = sem("s_ready"), sem("max_done"), sem("exp_done")
        pt_ready, hi_done, lo_done = sem("pt_ready"), sem("hi_done"), sem("lo_done")
        pv_done, inv_done, o_done = sem("pv_done"), sem("inv_done"), sem("o_done")
        row_ps, row_sb, row_used, lists, listed = sem("row_ps"), sem("row_sb"), sem("row_used"), sem("lists"), sem("listed")
        gathered = [sem(f"gathered{i}") for i in range(E // 2)]
        pair_in = sem("pair_in")
        tt_ps, xgT_s = sem("tt_ps"), sem("xgT")
        b_ps, tanh_s, silu_s = sem("b_ps"), sem("tanh_b"), sem("silu")
        a_ps, hid_s, hid_hi, hid_lo = sem("a_ps"), sem("hid"), sem("hid_hi"), sem("hid_lo")
        y_ps, y_s, added = sem("y_ps"), sem("y"), sem("added")
        sum_in = [sem(f"sum_in{i}") for i in range(2)]
        final, out_s = sem("final"), sem("out")

        XT_CREDIT, UNIT_CREDIT, PV_CREDIT, O_CREDIT, ROW_CREDIT, USED_CREDIT, Y_CREDIT = 2, 4, 1, 1, 1, 4, 1

        x_t = x.rearrange("b (n p) d -> p (b n) d", p=P)
        out_t = out.rearrange("b (n p) d -> p (b n) d", p=P)
        sum_t = sum_dram.rearrange("(n p) d -> p n d", p=P)
        xg_t = xg_dram.rearrange("(n p) c -> p n c", p=P)

        block = ctx.enter_context(nc.Block())

        @block.sync
        def _(sp):
            for b in range(B):
                sp.dma_start(x_sb[:, b * BT:(b + 1) * BT, :], x_t[:, b * BT:(b + 1) * BT, :]).then_inc(x_in[b], 16)
            for b in range(B):
                sp.wait_ge(x_lo, 2 * (b + 1))
                sp.dma_start(xg_t[:, b * BT:(b + 1) * BT, :], xhl[:, b * BT:(b + 1) * BT, :]).then_inc(xg_out, 16)
            for b in range(B):
                sp.wait_ge(xb_s, b + 1)
                sp.dma_start(sum_t[:, b * BT:(b + 1) * BT, :], x_sb[:, b * BT:(b + 1) * BT, :]).then_inc(xb_out, 16)
            sp.dma_start(sum_t[:, NT:NT + CB, :], x_sb[:, 0:CB, :]).then_inc(xb_out, 16)
            sp.wait_ge(added, 16 * NS)
            m = (ITS - 1) * STEPS
            sp.dma_start(x_sb[:, 0:m, :], sum_t[:, 0:m, :]).then_inc(sum_in[0], 16)
            sp.dma_start(x_sb[:, m:NT, :], sum_t[:, m:NT, :]).then_inc(sum_in[1], 16)
            for it in range(ITS - 1):
                t = it * STEPS
                sp.wait_ge(final, it + 1)
                sp.dma_start(out_t[:, t:t + STEPS, :], attn[:, t:t + STEPS, :]).then_inc(out_s, 16)
            for s in range(STEPS):
                t = m + s
                sp.wait_ge(o_done, t + 1 + O_CREDIT)
                sp.dma_start(out_t[:, t, :], attn[:, t, :]).then_inc(out_s, 16)
            sp.wait_ge(out_s, 16 * (ITS - 1 + STEPS))
            sp.wait_ge(xg_out, 16 * B)

        @block.scalar
        def _(act):
            act.dma_start(qkv_in[:], w_qkv).then_inc(small_in, 16)
            act.dma_start(owT_in[:], out_wT).then_inc(small_in, 16)
            act.dma_start(rw_in[:], router_wT).then_inc(small_in, 16)
            act.dma_start(rb[:], router_b.rearrange("(a e) -> a e", a=1).to_broadcast([P, E])).then_inc(small_in, 16)
            act.dma_start(bias[:], out_b.rearrange("(a d) -> a d", a=1).to_broadcast([P, D])).then_inc(small_in, 16)
            act.dma_start(wv_in[:, :, 0:H], w_in.rearrange("e d h -> d e h")).then_inc(w_in_s, 16)
            act.dma_start(wv_in[:, :, H:2 * H], v_in.rearrange("e d h -> d e h")).then_inc(w_in_s, 16)
            act.dma_start(wo_in[:].rearrange("p e (c d) -> p e c d", c=HB),
                          w_out.rearrange("e (c p) d -> p e c d", p=P)).then_inc(wo_in_s, 16)
            act.preload_act_table(ACT.Sqrt)

            def std_of(b):
                act.wait_ge(var_s, b + 1)
                act.activation(std[:, b * BT:(b + 1) * BT], mv[:, b * BT:(b + 1) * BT, 1], ACT.Sqrt).then_inc(std_s, 1)

            def x_high(b):
                for h in range(2):
                    t = b * BT + h * G
                    act.wait_ge(xn_s, b + 1)
                    act.activation(xhl[:, t:t + G, 0:D], probs[:, b % 2, h * GC:(h + 1) * GC].rearrange(
                        "p (n d) -> p n d", n=G), ACT.Copy).then_inc(x_hi, 1)

            def turned(b):
                for h in range(2):
                    g = 2 * b + h
                    act.wait_ge(xT_ps, g + 1)
                    act.activation(xT[:, :, g * GC:(g + 1) * GC], psT[:, h, :].bitcast(F16).rearrange(
                        "p (s c) -> p s c", s=2), ACT.Copy).then_inc(xT_s, 1)

            std_of(0)
            act.wait_ge(small_in, 80)
            act.activation(w_all[:], qkv_in[:], ACT.Copy, scale=W_SCALE).then_inc(small_w, 1)
            act.activation(owT[:, HI, :], owT_in[:], ACT.Copy, scale=W_SCALE).then_inc(small_w, 1)
            act.activation(rw[:, HI, :], rw_in[:], ACT.Copy, scale=W_SCALE).then_inc(small_w, 1)
            std_of(1)
            x_high(0)
            std_of(2)
            x_high(1)
            turned(0)
            std_of(3)
            x_high(2)
            turned(1)
            x_high(3)
            turned(2)
            turned(3)
            act.preload_act_table(ACT.Exp)
            act.wait_ge(gap_s, 1)
            act.activation(egap[:], gap[:], ACT.Exp).then_inc(egap_s, 1)

            def unit_high(bank, dst, scale):
                act.activation(dst, bank, ACT.Copy, scale=scale).then_inc(unit_hi, 1)

            with act.Fori(0, B) as b:
                for c in range(4):
                    act.wait_ge(unit_ps, 4 * b + c + 1)
                    at = bass.ds((2 * b + c // 2) * GC, GC)
                    dst, scale = (vT[:, HI, at], V_EVAC) if c % 2 == 0 else (kT[:, HI, at], K_EVAC)
                    unit_high(psS[:, c // 2, c % 2, :], dst, scale)
            act.wait_ge(gates_ps, 1)
            act.activation(row_src[:, 0:4, P:2 * P], psO[0:NT, :].rearrange("p (e t) -> p e t", e=4), ACT.Copy).then_inc(row_hi, 1)
            act.activation(row_src[:, 4:8, P:2 * P], psM[0:NT, :].rearrange("p (e t) -> p e t", e=4), ACT.Copy).then_inc(row_hi, 1)
            with act.Fori(0, B) as b:
                for c in range(4):
                    act.wait_ge(unit_ps, 4 * b + c + 1 + 4 * B)
                    g = 2 * b + c // 2
                    if c % 2 == 0:
                        unit_high(psS[:, c // 2, 0, :], qT[:, HI, bass.ds(g * GC, GC)], Q_EVAC)
                    else:
                        unit_high(psS[:, c // 2, 1, :].rearrange("p (n d) -> p n d", n=G), vp[:, bass.ds(g * G, G), HI, :], V_EVAC)

            def exp_of(i, par):
                act.wait_ge(max_done, i + 1)
                act.activation(probs[:, par % 2, :], psS[:, par % 2].rearrange("p a c -> p (a c)"), ACT.Exp,
                               bias=neg_max[:, par % 4:par % 4 + 1],
                               accum_out=row_sum[:, par % 4:par % 4 + 1]).then_inc(exp_done, 1)

            def probs_high(i, par):
                for h in range(2):
                    act.wait_ge(pt_ready, 2 * i + h + 1)
                    if h == 0:
                        act.wait_ge(pv_done, i - 1 + PV_CREDIT)
                    act.activation(pT[:, par % 2, HI, h * 512:(h + 1) * 512], psT[:, h, :], ACT.Copy).then_inc(hi_done, 1)

            def row_out(e, s, j):
                u = 2 * e + j
                act.wait_ge(row_ps, u + 1)
                act.wait_ge(row_used, u + 1 - 4 + USED_CREDIT)
                act.activation(row[:, (2 * s + j) % 4, :], psM[:, 0:RC], ACT.Copy).then_inc(row_sb, 1)

            def tanh_of(e):
                act.wait_ge(b_ps, e + 1)
                act.activation(tanh_b, psM[:], ACT.Tanh, scale=0.5 / W_SCALE).then_inc(tanh_s, 1)

            def hid_high(e, q):
                act.wait_ge(hid_s, e + 1)
                act.activation(hidT[:, q, HI, :], hid[:, q, :], ACT.Copy).then_inc(hid_hi, 1)

            def y_out(e):
                act.wait_ge(y_ps, e + 1)
                for j in range(CB):
                    ins = act.activation(y_sb[:, bass.ds(2 * e + j, 1), :].rearrange("p a d -> p (a d)"),
                                         psM[:, j * D:(j + 1) * D], ACT.Copy,
                                         scale=slot_ws[:, bass.ds(2 * e + j, 1)])
                ins.then_inc(y_s, 1)

            def steps(it, lists=False, experts=False, last=False):
                for s in range(STEPS):
                    i = it * STEPS + s
                    e0 = 2 * (it - 2)
                    if lists:
                        row_out(4 * it + s, s, 0)
                    if experts and s in (1, 2):
                        tanh_of(e0 + s - 1)
                    if not last or s < STEPS - 1:
                        probs_high(i + 1, s + 1)
                    if experts and s == 3:
                        y_out(e0)
                        hid_high(e0 + 1, 1)
                    if not last or s < STEPS - 2:
                        exp_of(i + 2, s + 2)
                    if lists:
                        row_out(4 * it + s, s, 1)
                    if experts and s == 2:
                        hid_high(e0, 0)
                    if experts and s == 3:
                        y_out(e0 + 1)

            exp_of(0, 0)
            exp_of(1, 1)
            for h in range(2):
                act.wait_ge(pt_ready, h + 1)
                act.activation(pT[:, 0, HI, h * 512:(h + 1) * 512], psT[:, h, :], ACT.Copy).then_inc(hi_done, 1)
            act.wait_ge(w_in_s, 32)
            for c in range(4):
                ce = slice(2 * c, 2 * c + 2)
                act.activation(wv[:, HI, ce, :], wv_in[:, ce, :], ACT.Copy, scale=W_SCALE).then_inc(wv_hi, 1)
            with act.Fori(0, 2) as it:
                steps(it, lists=True)
            with act.Fori(2, 6) as it:
                steps(it, experts=True)
            steps(6)
            steps(7, last=True)

        @block.vector
        def _(dve):
            dve.memset(w_mid[:], 0.0).then_inc(zeroed, 1)
            dve.memset(neg_max[:], 0.0).then_inc(xT_s, XT_CREDIT)
            dve.memset(row_sum[:], 0.0).then_inc(unit_lo, UNIT_CREDIT)
            dve.memset(inv_sum[:], 0.0).then_inc(pv_done, PV_CREDIT)
            dve.memset(count[:], 0.0).then_inc(o_done, O_CREDIT)
            dve.memset(aux[:], 0.0).then_inc(row_sb, ROW_CREDIT)
            dve.memset(slot_w[:], 0.0).then_inc(row_used, USED_CREDIT)
            dve.memset(unused[:], 0.0).then_inc(y_s, Y_CREDIT)

            def stats_of(b):
                dve.wait_ge(x_in[b], 16)
                for t in range(b * BT, (b + 1) * BT):
                    ins = dve.bn_stats(stats[:, t, :], x_sb[:, t, :])
                ins.then_inc(stat_s, 1)
                dve.wait_ge(stat_s, 2 * b + 1)
                for t in range(b * BT, (b + 1) * BT):
                    ins = dve.bn_aggr(mv[:, t, :], stats[:, t, :])
                ins.then_inc(stat_s, 1)
                dve.wait_ge(stat_s, 2 * b + 2)
                v = mv[:, b * BT:(b + 1) * BT, 1]
                dve.tensor_scalar(v, v, EPS, None, ALU.add).then_inc(var_s, 1)

            def normalise(b):
                dve.wait_ge(std_s, b + 1)
                dve.reciprocal(rstd[:, b * BT:(b + 1) * BT], std[:, b * BT:(b + 1) * BT]).then_inc(rstd_s, 1)
                dve.wait_ge(rstd_s, b + 1)
                if b >= 2:
                    dve.wait_ge(x_lo, 2 * (b - 1))
                for k in range(BT):
                    t = b * BT + k
                    ins = dve.tensor_scalar(probs[:, b % 2, k * D:(k + 1) * D], x_sb[:, t, :], mv[:, t, 0:1],
                                            rstd[:, t:t + 1], ALU.subtract, ALU.mult)
                ins.then_inc(xn_s, 1)

            stats_of(0)
            stats_of(1)
            normalise(0)
            stats_of(2)
            normalise(1)
            dve.wait_ge(consts_i, 4)
            dve.tensor_copy(slot_row[:], slot_i[0:NT, :])
            dve.tensor_copy(slot_col[:], slot_col_i[:])
            dve.tensor_scalar(slot_next[:], slot_col_i[:], 1.0, None, ALU.add)
            dve.tensor_scalar(slot_dump[:], slot_col_i[:], float(N - P), None, ALU.add)
            dve.tensor_copy(rank[:], rank_i[:])
            for e in range(E):
                ins = dve.tensor_copy(row_src[:, e, 2 * P:RC], tile_i[:])
            ins.then_inc(consts, 1)
            dve.wait_ge(small_w, 3)
            dve.wait_ge(zeroed, 1)
            for m0 in (LOW, 2 * LOW):
                mid = slice(m0, m0 + LOW)
                dve.tensor_copy(w_mid[mid, HI, :], w_all[mid, :]).then_inc(small_w, 1)
                dve.scalar_tensor_tensor(out=w_mid[mid, LO, :], in0=qkv_in[mid, :], scalar=W_SCALE, in1=w_all[mid, :],
                                         op0=ALU.mult, op1=ALU.subtract).then_inc(small_w, 1)
            dve.scalar_tensor_tensor(out=owT[:, LO, :], in0=owT_in[:], scalar=W_SCALE, in1=owT[:, HI, :],
                                     op0=ALU.mult, op1=ALU.subtract).then_inc(small_w, 1)
            dve.scalar_tensor_tensor(out=rw[:, LO, :], in0=rw_in[:], scalar=W_SCALE, in1=rw[:, HI, :],
                                     op0=ALU.mult, op1=ALU.subtract).then_inc(small_w, 1)
            stats_of(3)
            normalise(2)
            normalise(3)

            n = [0]

            def then(ins):
                n[0] += 1
                ins.then_inc(route, 1)
                dve.wait_ge(route, n[0])

            def over_e(a):
                return a[:].unsqueeze(2).to_broadcast([P, NT, E])

            rank_b = rank[:].unsqueeze(1).to_broadcast([P, NT, E])
            rb_b = rb[:].unsqueeze(1).to_broadcast([P, NT, E])
            dve.wait_ge(scores_r, NG)
            dve.wait_ge(consts, 1)
            then(dve.scalar_tensor_tensor(out=logits, in0=psM[:, 0:NT * E].rearrange("p (n e) -> p n e", e=E),
                                          scalar=1.0 / W_SCALE, in1=rb_b, op0=ALU.mult, op1=ALU.add))
            then(dve.tensor_reduce(top1[:], logits, AX, ALU.max))
            then(dve.tensor_tensor(ta[:], logits, over_e(top1), ALU.is_equal))
            then(dve.tensor_tensor(ta[:], ta[:], rank_b, ALU.mult))
            then(dve.tensor_reduce(pick[:], ta[:], AX, ALU.max))
            then(dve.tensor_tensor(first, rank_b, over_e(pick), ALU.is_equal))
            then(dve.scalar_tensor_tensor(out=rest, in0=first, scalar=-BIG, in1=logits, op0=ALU.mult, op1=ALU.add))
            then(dve.tensor_reduce(top2[:], rest, AX, ALU.max))
            dve.tensor_tensor(gap[:], top2[:], top1[:], ALU.subtract).then_inc(gap_s, 1)
            then(dve.tensor_tensor(ta[:], rest, over_e(top2), ALU.is_equal))
            then(dve.tensor_tensor(ta[:], ta[:], rank_b, ALU.mult))
            then(dve.tensor_reduce(pick[:], ta[:], AX, ALU.max))
            then(dve.tensor_tensor(second, rank_b, over_e(pick), ALU.is_equal))
            dve.tensor_tensor(mask[:], first, second, ALU.add).then_inc(plan_in, 1)
            dve.wait_ge(egap_s, 1)
            then(dve.tensor_scalar(pick[:], egap[:], 1.0, None, ALU.add))
            then(dve.reciprocal(gate1[:], pick[:]))
            then(dve.tensor_tensor(gate2[:], gate1[:], egap[:], ALU.mult))
            then(dve.tensor_tensor(first, first, over_e(gate1), ALU.mult))
            then(dve.tensor_tensor(second, second, over_e(gate2), ALU.mult))
            dve.tensor_tensor(ta[:], first, second, ALU.add).then_inc(plan_in, 1)

            def unit_low(bank, hi, lo, scale, done):
                dve.wait_ge(unit_hi, done)
                dve.scalar_tensor_tensor(out=lo, in0=bank, scalar=scale, in1=hi, op0=ALU.mult,
                                         op1=ALU.subtract).then_inc(unit_lo, 1)

            with dve.Fori(0, B) as b:
                for c in range(4):
                    at = bass.ds((2 * b + c // 2) * GC, GC)
                    dst, scale = (vT, V_EVAC) if c % 2 == 0 else (kT, K_EVAC)
                    unit_low(psS[:, c // 2, c % 2, :], dst[:, HI, at], dst[:, LO, at], scale, 4 * b + c + 1)

            dve.wait_ge(counts_ps, 1)
            counts = psT[0:NT].rearrange("p a (e t) -> p (a e) t", e=4)
            dve.tensor_copy(tot[:], counts[:, :, P - 1]).then_inc(tot_s, 1)
            dve.wait_ge(row_hi, 2)
            dve.tensor_tensor(row_lo[:, 0:4, :], psO[0:NT, :].rearrange("p (e t) -> p e t", e=4),
                              row_src[:, 0:4, P:2 * P], ALU.subtract).then_inc(row_lo_s, 1)
            dve.tensor_tensor(row_lo[:, 4:8, :], psM[0:NT, :].rearrange("p (e t) -> p e t", e=4),
                              row_src[:, 4:8, P:2 * P], ALU.subtract).then_inc(row_lo_s, 1)
            dve.wait_ge(start_ps, 1)
            dve.tensor_copy(start[:], psO[0:NT, 0:E])
            dve.wait_ge(tot_s, 1)
            then(dve.tensor_tensor(end[:], psO[0:NT, 0:E], tot[:], ALU.add))
            for e in range(E):
                dve.tensor_scalar(row_src[:, e, 0:P], counts[:, e, :], start[:, e:e + 1], 2.0 * CAP, ALU.add, ALU.min)
                ins = dve.tensor_scalar(before_end[:, e, :], slot_row[:], end[:, e:e + 1], None, ALU.is_lt)
            then(ins)
            for e in range(E):
                ins = dve.scalar_tensor_tensor(out=in_tile[:, e, :], in0=slot_row[:], scalar=start[:, e:e + 1],
                                               in1=before_end[:, e, :], op0=ALU.is_ge, op1=ALU.mult)
            ins.then_inc(plan_s, 1)

            with dve.Fori(0, B) as b:
                for c in range(4):
                    g = 2 * b + c // 2
                    if c % 2 == 0:
                        at = bass.ds(g * GC, GC)
                        unit_low(psS[:, c // 2, 0, :], qT[:, HI, at], qT[:, LO, at], Q_EVAC, 4 * b + c + 1 + 4 * B)
                    else:
                        at = bass.ds(g * G, G)
                        unit_low(psS[:, c // 2, 1, :].rearrange("p (n d) -> p n d", n=G), vp[:, at, HI, :],
                                 vp[:, at, LO, :], V_EVAC, 4 * b + c + 1 + 4 * B)

            def max_of(i, par):
                dve.wait_ge(s_ready, i + 1)
                dve.tensor_reduce(neg_max[:, par % 4:par % 4 + 1], psS[:, par % 2].rearrange("p a c -> p (a c)"),
                                  AX, ALU.max, negate=True).then_inc(max_done, 1)

            def probs_low(i, par):
                for h in range(2):
                    cols = slice(h * 512, (h + 1) * 512)
                    dve.wait_ge(hi_done, 2 * i + h + 1)
                    dve.tensor_tensor(pT[:, par % 2, LO, cols], psT[:, h, :], pT[:, par % 2, HI, cols],
                                      ALU.subtract).then_inc(lo_done, 1)

            def scale_out(i, par, last):
                c = slice(par % 4, par % 4 + 1)
                dve.wait_ge(exp_done, i + 1)
                dve.reciprocal(inv_sum[:, c], row_sum[:, c]).then_inc(inv_done, 1)
                dve.wait_ge(inv_done, i + 1)
                dve.wait_ge(pv_done, i + 1 + PV_CREDIT)
                if last:
                    dve.wait_ge(sum_in[1], 16)
                    dve.scalar_tensor_tensor(out=attn[:, i, :], in0=psO[:, 0:D], scalar=inv_sum[:, c],
                                             in1=x_sb[:, i, :], op0=ALU.mult, op1=ALU.add).then_inc(o_done, 1)
                else:
                    dve.tensor_scalar(attn[:, bass.ds(i, 1), :].rearrange("p a d -> p (a d)"), psO[:, 0:D],
                                      inv_sum[:, c], None, ALU.mult).then_inc(o_done, 1)

            def row_read(e, s, j):
                u = 2 * e + j
                r = row[:, (2 * s + j) % 4, :]
                dve.wait_ge(row_sb, u + 1 + ROW_CREDIT)
                dve.scalar_tensor_tensor(out=r[:, P:2 * P], in0=r[:, 0:P], scalar=slot_next[:, j:j + 1],
                                         in1=r[:, P:2 * P], op0=ALU.is_equal, op1=ALU.mult,
                                         accum_out=slot_w[:, bass.ds(u, 1)])
                dve.tensor_scalar(r[:, 0:P], r[:, 0:P], slot_col[:, j:j + 1], None, ALU.is_le, ALU.add,
                                  accum_out=count[:, bass.ds(u, 1)])
                dve.tensor_copy(aux[:, bass.ds(u, 1), :].rearrange("p a c -> p (a c)"), r[:, 2 * P:RC]).then_inc(row_used, 1)

            def gate_of(e):
                dve.wait_ge(tanh_s, e + 1)
                dve.scalar_tensor_tensor(out=silu, in0=tanh_b, scalar=1.0, in1=psM[:], op0=ALU.add,
                                         op1=ALU.mult).then_inc(silu_s, 1)

            def hidden_of(e, q):
                dve.wait_ge(a_ps, e + 1)
                dve.wait_ge(silu_s, e + 1)
                dve.scalar_tensor_tensor(out=hid[:, q, :], in0=psM[:], scalar=0.5 / (W_SCALE * W_SCALE), in1=silu,
                                         op0=ALU.mult, op1=ALU.mult).then_inc(hid_s, 1)

            def steps(it, lists=False, experts=False, last=False):
                for s in range(STEPS):
                    i = it * STEPS + s
                    e0 = 2 * (it - 2)
                    if experts and s in (2, 3):
                        hidden_of(e0 + s - 2, s - 2)
                    if not last or s < STEPS - 2:
                        max_of(i + 2, s + 2)
                    if experts and s in (1, 2):
                        gate_of(e0 + s - 1)
                    if not last or s < STEPS - 1:
                        probs_low(i + 1, s + 1)
                    if lists:
                        row_read(4 * it + s, s, 0)
                    scale_out(i, s, last)
                    if lists:
                        row_read(4 * it + s, s, 1)
                    if experts and s == 0:
                        dve.wait_ge(tt_ps, it - 2 + 1)
                        dve.tensor_copy(xgT, psM[:].bitcast(F16).rearrange("p (q s c) -> p q s c", q=2, s=2)).then_inc(xgT_s, 1)

            max_of(0, 0)
            max_of(1, 1)
            probs_low(0, 0)
            with dve.Fori(0, 2) as it:
                steps(it, lists=True)
            dve.wait_ge(row_used, NS + USED_CREDIT)
            dve.tensor_scalar(unused[:], aux[:, :, 1], -1.0, 1.0, ALU.mult, ALU.add)
            then(dve.tensor_tensor(where[:], aux[:, :, 0], count[:], ALU.add))
            dve.tensor_scalar(slot_ws[:], slot_w[:], 1.0 / W_SCALE, None, ALU.mult).then_inc(listed, 1)
            then(dve.tensor_tensor(unused[:], unused[:], slot_dump[:], ALU.mult))
            then(dve.tensor_tensor(where[:], where[:], unused[:], ALU.add))
            dve.tensor_scalar(from_row[:], where[:], float(N - 1), None, ALU.min).then_inc(listed, 1)
            dve.tensor_copy(to_row[:], where[:]).then_inc(listed, 1)
            with dve.Fori(2, 6) as it:
                steps(it, experts=True)
            steps(6)
            steps(7, last=True)

        @block.gpsimd
        def _(pool):
            pool.iota(slot_i[:], [[1, CAP]], base=0, channel_multiplier=0).then_inc(consts_i, 1)
            pool.iota(slot_col_i[:].rearrange("p (e j) -> p e j", j=CB), [[0, E], [P, CB]], base=0,
                      channel_multiplier=1).then_inc(consts_i, 1)
            pool.iota(rank_i[:], [[-1, E]], base=E, channel_multiplier=0).then_inc(consts_i, 1)
            pool.memset(ident16[:], 0.0).then_inc(zeroed, 1)
            pool.memset(ident[:], 0.0).then_inc(zeroed, 1)
            pool.memset(upper[:], 1.0).then_inc(zeroed, 1)
            pool.memset(below[:], 1.0).then_inc(zeroed, 1)
            pool.memset(tile_i[:], 1).then_inc(zeroed, 1)
            pool.wait_ge(zeroed, 6)
            pool.iota(tile_i[:, 0:1], [[0, 1]], base=0, channel_multiplier=P).then_inc(consts_i, 1)
            for t in (ident16, ident):
                pool.affine_select(out=t[:], in_=t[:], compare_op=ALU.not_equal, fill=1.0, base=0, pattern=[[-1, P]],
                                   channel_multiplier=1).then_inc(consts_i, 1)
            pool.affine_select(out=upper[:], in_=upper[:], compare_op=ALU.is_ge, fill=0.0, base=0, pattern=[[1, P]],
                               channel_multiplier=-1).then_inc(consts_i, 1)
            pool.affine_select(out=below[:], in_=below[:], compare_op=ALU.is_gt, fill=0.0, base=0, pattern=[[1, NT]],
                               channel_multiplier=-1).then_inc(consts_i, 1)
            for b in range(B):
                for h in range(2):
                    t = b * BT + h * G
                    pool.wait_ge(x_hi, 2 * b + h + 1)
                    pool.tensor_tensor(xhl[:, t:t + G, D:2 * D], probs[:, b % 2, h * GC:(h + 1) * GC].rearrange(
                        "p (n d) -> p n d", n=G), xhl[:, t:t + G, 0:D], ALU.subtract).then_inc(x_lo, 1)
            pool.wait_ge(small_in, 80)
            bias_b = bias[:].unsqueeze(1).to_broadcast([P, BT, D])
            for b in range(B):
                xb = x_sb[:, b * BT:(b + 1) * BT, :]
                pool.tensor_tensor(xb, xb, bias_b, ALU.add).then_inc(xb_s, 1)
            pool.wait_ge(wo_in_s, 16)
            pool.tensor_scalar(wo_in[:], wo_in[:], W_SCALE, 0.0, ALU.mult, ALU.add).then_inc(w_up, 1)
            pool.wait_ge(w_up, 1)
            pool.tensor_scalar(wo[:, HI], wo_in[:], 1.0, 0.0, ALU.mult, ALU.add).then_inc(wo_hi, 1)
            pool.wait_ge(wo_hi, 1)
            pool.tensor_tensor(wo[:, LO], wo_in[:], wo[:, HI], ALU.subtract).then_inc(wo_lo, 1)
            pool.wait_ge(w_in_s, 32)
            for c in range(4):
                ce = slice(2 * c, 2 * c + 2)
                pool.wait_ge(wv_hi, c + 1)
                pool.tensor_scalar(wv_in[:, ce, :], wv_in[:, ce, :], W_SCALE, 0.0, ALU.mult, ALU.add).then_inc(w_up, 1)
                pool.wait_ge(w_up, c + 2)
                pool.tensor_tensor(wv[:, LO, ce, :], wv_in[:, ce, :], wv[:, HI, ce, :], ALU.subtract).then_inc(wv_lo, 1)
            pool.wait_ge(listed, 3)
            pool.wait_ge(xg_out, 16 * B)
            pool.wait_ge(wv_lo, 4)
            for k in range(NS):
                pool.indirect_dma_start(xg[:, k, :], None, xg_dram[:, :],
                                        bass.IndirectOffsetOnAxis(ap=from_row[:, k:k + 1], axis=0),
                                        bounds_check=N - 1, oob_is_err=True).then_inc(gathered[k // 4], 16)
            for i in range(E // 2):
                pool.wait_ge(gathered[i], 64)
                pool.sem_inc(pair_in, 1)
            pool.wait_ge(xb_out, 16 * (B + 1))
            for e in range(E):
                pool.wait_ge(hid_s, e + 1)
                pool.wait_ge(hid_hi, e + 1)
                pool.tensor_tensor(hidT[:, e % 2, LO, :], hid[:, e % 2, :], hidT[:, e % 2, HI, :],
                                   ALU.subtract).then_inc(hid_lo, 1)
                if e % 2 == 0:
                    continue
                for ee in (e - 1, e):
                    pool.wait_ge(y_s, ee + 1 + Y_CREDIT)
                    if ee > 0:
                        pool.wait_ge(added, 16 * CB * ee)
                    for j in range(CB):
                        k = ee * CB + j
                        pool.indirect_dma_start(sum_dram[:, :], bass.IndirectOffsetOnAxis(ap=to_row[:, k:k + 1], axis=0),
                                                y_sb[:, k, :], None, bounds_check=N + CAP - 1, oob_is_err=True,
                                                compute_op=ALU.add).then_inc(added, 16)
            pool.wait_ge(sum_in[0], 16)
            for it in range(ITS - 1):
                t = slice(it * STEPS, (it + 1) * STEPS)
                pool.wait_ge(o_done, (it + 1) * STEPS + O_CREDIT)
                pool.tensor_tensor(attn[:, t, :], attn[:, t, :], x_sb[:, t, :], ALU.add).then_inc(final, 1)

        @block.tensor
        def _(pe):
            def mm(o, a, b, first, last):
                return pe.matmul(o, a, b, start=first, stop=last)

            pe.wait_ge(consts_i, 8)
            pe.wait_ge(small_w, 9)

            with pe.Fori(0, B) as b:
                for h in range(2):
                    g = 2 * b + h
                    pe.wait_ge(x_lo, g + 1)
                    pe.wait_ge(xT_s, g + 1 - 2 + XT_CREDIT)
                    bank = psT[:, h, :].bitcast(F16)
                    for s in (HI, LO):
                        for t in range(G):
                            ins = pe.transpose(bank[:, (s * G + t) * P:(s * G + t + 1) * P],
                                               xhl[:, bass.ds(g * G + t, 1), s * D:(s + 1) * D].rearrange("p a d -> p (a d)"),
                                               ident16[:])
                    ins.then_inc(xT_ps, 1)
                for h in range(2):
                    g = 2 * b + h
                    pe.wait_ge(xT_s, g + 1 + XT_CREDIT)
                    for t in range(G):
                        o = psM[:, bass.ds((g * G + t) * E, E)]
                        at = bass.ds((g * G + t) * P, P)
                        mm(o, xT[:, HI, at], rw[:, HI, :], True, False)
                        mm(o, xT[:, HI, at], rw[:, LO, :], False, False)
                        ins = mm(o, xT[:, LO, at], rw[:, HI, :], False, True)
                    ins.then_inc(scores_r, 1)

            def project(bank, w, at):
                c = slice(w * D, (w + 1) * D)
                mm(bank, w_all[:, c], xT[:, HI, at], True, False)
                mm(bank, w_mid[:, LO, c], xT[:, HI, at], False, False)
                return mm(bank, w_mid[:, HI, c], xT[:, LO, at], False, True)

            with pe.Fori(0, B) as b:
                for c in range(4):
                    pe.wait_ge(unit_lo, 4 * b + c + 1 - 4 + UNIT_CREDIT)
                    at = bass.ds((2 * b + c // 2) * GC, GC)
                    project(psS[:, c // 2, c % 2, :], 2 - c % 2, at).then_inc(unit_ps, 1)
            pe.wait_ge(plan_in, 2)
            for e in range(E):
                ins = mm(psT[0:NT, e // 4, (e % 4) * P:(e % 4 + 1) * P], mask[:, :, e], upper[:], True, True)
            ins.then_inc(counts_ps, 1)
            for e in range(E):
                bank = psO if e < 4 else psM
                ins = pe.transpose(bank[0:NT, (e % 4) * P:(e % 4 + 1) * P], ta[:, :, e], ident[:])
            ins.then_inc(gates_ps, 1)
            pe.wait_ge(row_lo_s, 2)
            pe.wait_ge(tot_s, 1)
            mm(psO[0:NT, 0:E], below[:], tot[:], True, True).then_inc(start_ps, 1)
            with pe.Fori(0, B) as b:
                for c in range(4):
                    pe.wait_ge(unit_lo, 4 * b + c + 1 - 4 + UNIT_CREDIT + 4 * B)
                    g = 2 * b + c // 2
                    if c % 2 == 0:
                        ins = project(psS[:, c // 2, 0, :], 0, bass.ds(g * GC, GC))
                    else:
                        for t in range(G):
                            o = psS[:, c // 2, 1, t * D:(t + 1) * D]
                            at = bass.ds((g * G + t) * P, P)
                            mm(o, vT[:, HI, at], owT[:, HI, :], True, False)
                            mm(o, vT[:, HI, at], owT[:, LO, :], False, False)
                            ins = mm(o, vT[:, LO, at], owT[:, HI, :], False, True)
                    ins.then_inc(unit_ps, 1)

            def scores(i, batch, par):
                for c in range(2):
                    o = psS[:, par % 2, c, :]
                    at = bass.ds(i * P, P)
                    key = bass.ds(batch * T + c * 512, 512)
                    mm(o, qT[:, HI, at], kT[:, HI, key], True, False)
                    mm(o, qT[:, HI, at], kT[:, LO, key], False, False)
                    ins = mm(o, qT[:, LO, at], kT[:, HI, key], False, True)
                ins.then_inc(s_ready, 1)

            def turn_probs(i, par, first):
                pe.wait_ge(exp_done, i + 1)
                for h in range(2):
                    if not first:
                        pe.wait_ge(lo_done, 2 * (i - 1) + h + 1)
                    for k in range(4):
                        ins = pe.transpose(psT[:, h, k * P:(k + 1) * P], probs[:, par % 2, (4 * h + k) * P:(4 * h + k + 1) * P],
                                           ident[:])
                    ins.then_inc(pt_ready, 1)

            def weigh_values(i, batch, par):
                pe.wait_ge(lo_done, 2 * i + 2)
                pe.wait_ge(o_done, i + O_CREDIT)
                for k in range(BT):
                    ph, pl = (pT[:, par % 2, s, k * P:(k + 1) * P] for s in (HI, LO))
                    v_hi, v_lo = (vp[:, bass.ds(batch * BT + k, 1), s, :].rearrange("p a d -> p (a d)") for s in (HI, LO))
                    mm(psO[:, 0:D], ph, v_hi, k == 0, False)
                    mm(psO[:, 0:D], ph, v_lo, False, False)
                    ins = mm(psO[:, 0:D], pl, v_hi, False, k == BT - 1)
                ins.then_inc(pv_done, 1)

            def slot_rows(e, s, j):
                u = 2 * e + j
                pe.wait_ge(row_sb, u + ROW_CREDIT)
                a = in_tile[:, bass.ds(e, 1), j * P:(j + 1) * P].rearrange("p a c -> p (a c)")
                mm(psM[:, 0:RC], a, row_src[:, bass.ds(e, 1), :].rearrange("p a c -> p (a c)"), True, False)
                mm(psM[:, P:2 * P], a, row_lo[:, bass.ds(e, 1), :].rearrange("p a c -> p (a c)"), False,
                   True).then_inc(row_ps, 1)

            def turn_rows(p):
                pe.wait_ge(pair_in, p + 1)
                pe.wait_ge(y_s, 2 * p + Y_CREDIT)
                bank = psM[:].bitcast(F16)
                for q in range(2):
                    for s in (HI, LO):
                        for j in range(CB):
                            o = ((q * 2 + s) * CB + j) * P
                            ins = pe.transpose(bank[:, o:o + P], xg[:, bass.ds(4 * p + 2 * q + j, 1), s * D:(s + 1) * D]
                                               .rearrange("p a d -> p (a d)"), ident16[:])
                ins.then_inc(tt_ps, 1)

            def branch(e, q, off):
                for c in range(HB):
                    o = psM[:, c * CAP:(c + 1) * CAP]
                    wh, wl = (wv[:, s, bass.ds(e, 1), off + c * P:off + (c + 1) * P].rearrange("p a h -> p (a h)")
                              for s in (HI, LO))
                    mm(o, wh, xgT[:, q, HI, :], True, False)
                    mm(o, wl, xgT[:, q, HI, :], False, False)
                    ins = mm(o, wh, xgT[:, q, LO, :], False, True)
                return ins

            def expert_out(e, q):
                pe.wait_ge(hid_lo, e + 1)
                for j in range(CB):
                    o = psM[:, j * D:(j + 1) * D]
                    for c in range(HB):
                        hh, hl = (hidT[:, q, s, c * CAP + j * P:c * CAP + (j + 1) * P] for s in (HI, LO))
                        w_hi, w_lo = (wo[:, s, bass.ds(e, 1), c * D:(c + 1) * D].rearrange("p a d -> p (a d)")
                                      for s in (HI, LO))
                        mm(o, hh, w_hi, c == 0, False)
                        mm(o, hh, w_lo, False, False)
                        ins = mm(o, hl, w_hi, False, c == HB - 1)
                ins.then_inc(y_ps, 1)

            def steps(it, lists=False, experts=False, last=False):
                for s in range(STEPS):
                    i = it * STEPS + s
                    e0 = 2 * (it - 2)
                    if not last or s < STEPS - 2:
                        pe.wait_ge(exp_done, i + 1)
                        scores(i + 2, (it + s // 2) >> 1, s + 2)
                    if lists:
                        slot_rows(4 * it + s, s, 0)
                    if experts and s in (1, 2):
                        pe.wait_ge(xgT_s, it - 2 + 1)
                        if s == 2:
                            pe.wait_ge(hid_s, e0 + 1)
                        branch(e0 + s - 1, s - 1, H).then_inc(b_ps, 1)
                    if experts and s == 3:
                        pe.wait_ge(hid_s, e0 + 2)
                        expert_out(e0, 0)
                    if not last or s < STEPS - 1:
                        turn_probs(i + 1, s + 1, False)
                    weigh_values(i, it >> 1, s)
                    if lists:
                        slot_rows(4 * it + s, s, 1)
                    if experts and s == 0:
                        turn_rows(it - 2)
                    if experts and s in (1, 2):
                        pe.wait_ge(silu_s, e0 + s)
                        branch(e0 + s - 1, s - 1, 0).then_inc(a_ps, 1)
                    if experts and s == 3:
                        pe.wait_ge(y_s, e0 + 1 + Y_CREDIT)
                        expert_out(e0 + 1, 1)

            pe.wait_ge(unit_lo, 8 * B + UNIT_CREDIT)
            scores(0, 0, 0)
            scores(1, 0, 1)
            pe.wait_ge(plan_s, 1)
            turn_probs(0, 0, True)
            with pe.Fori(0, 2) as it:
                steps(it, lists=True)
            pe.wait_ge(row_sb, NS + ROW_CREDIT)
            pe.wait_ge(wo_lo, 1)
            pe.wait_ge(wv_lo, 4)
            with pe.Fori(2, 6) as it:
                steps(it, experts=True)
            steps(6)
            steps(7, last=True)


_INS = ["x", "w_qkv", "out_wT", "out_b", "router_wT", "router_b", "w_in", "v_in", "w_out"]


def kernel(L0_attn_x, L0_attn_weight_qkv, L0_attn_out_w, L0_attn_out_b, L0_ffn_router_w, L0_ffn_router_b,
           L0_ffn_W, L0_ffn_V, L0_ffn_W_out):
    import numpy as _np
    import concourse.bacc as _bacc
    from concourse import mybir as _mybir
    from concourse.bass_utils import run_bass_kernel_spmd as _run

    given = [L0_attn_x, L0_attn_weight_qkv, _np.asarray(L0_attn_out_w).T, L0_attn_out_b,
             _np.asarray(L0_ffn_router_w).T, L0_ffn_router_b, L0_ffn_W, L0_ffn_V, L0_ffn_W_out]
    nc = _bacc.Bacc("TRN2", target_bir_lowering=False, num_devices=1)
    arrays, args = {}, []
    for name, a in zip(_INS, given):
        a = _np.ascontiguousarray(a)
        arrays[f"in_{name}"] = a
        args.append(nc.dram_tensor(f"in_{name}", a.shape, _mybir.dt.from_np(a.dtype), kind="ExternalInput").ap())
    args.append(nc.dram_tensor("out", arrays["in_x"].shape, F32, kind="ExternalOutput").ap())
    block_kernel(nc, *args)
    r = _run(nc, [arrays], core_ids=[0])
    return r.results[0]["out"]
```

```python
from contextlib import ExitStack

import concourse.bass as bass
from concourse import mybir

F32 = mybir.dt.float32
F16 = mybir.dt.float16
I32 = mybir.dt.int32
ALU = mybir.AluOpType
ACT = mybir.ActivationFunctionType
AX = mybir.AxisListType.X

P = 128
EPS = 1e-5
HI, LO = 0, 1
W_SCALE = 64.0
BIG = 3.0e38
STEPS = 4


def block_kernel(nc, x, w_qkv, out_wT, out_b, router_wT, router_b, w_in, v_in, w_out, out):
    B, T, D = x.shape
    N = B * T
    NT = N // P
    BT = T // P
    E, _, H = w_in.shape
    HB = H // P
    CAP = 2 * 512 * 2 // E
    CB = CAP // P
    NS = E * CB
    LOW = D // 4
    G = 4
    NG = NT // G
    ITS = NT // STEPS
    GC = G * P
    EB = P // NT
    NB = E // EB
    RC = 2 * P + 2
    assert NS // 2 == EB * CB and EB == STEPS and D == P and HB == 2 and CB == 2 and BT == 8 and B == 4

    Q_EVAC = 4.0 / (float(D) ** 0.5 * W_SCALE)
    K_SCALE = 1.0 / 4.0
    V_EVAC = 1.0 / W_SCALE

    xg_dram = nc.dram_tensor("xn_hi_lo", (N, 2 * D), F16, kind="Internal").ap()
    sum_dram = nc.dram_tensor("x_bias_experts", (N + CAP, D), F32, kind="Internal").ap()

    with ExitStack() as ctx:
        def sb(name, shape, dt=F32):
            return ctx.enter_context(nc.sbuf_tensor(name, shape, dt))

        def psum(name, shape):
            return ctx.enter_context(nc.psum_tensor(name, shape, F32))

        def sem(name):
            return ctx.enter_context(nc.semaphore(name))

        psS = psum("psS", [P, 2, 2, 512])
        psT = psum("psT", [P, 2, 512])
        psO = psum("psO", [P, 512])
        psM = psum("psM", [P, 512])

        x_sb = sb("x_sb", [P, NT, D])
        probs = sb("probs", [P, 2, T])
        xhl = sb("xhl", [P, NT, 2 * D], F16)
        xT = sb("xT", [P, 2, N], F16)
        qT = sb("qT", [P, 2, N], F16)
        kT = sb("kT", [P, 2, N], F16)
        vp = sb("vp", [P, NT, 2, D], F16)
        attn = sb("attn", [P, NT, D])
        attn_flat = attn[:].rearrange("p n d -> p (n d)")
        qkv_in = attn_flat[:, 0:3 * D]
        owT_in = attn_flat[:, 3 * D:4 * D]
        w_hl, wT = (attn_flat[:, c * D:(c + 3) * D].bitcast(F16).rearrange("p (s c) -> p s c", s=2) for c in (4, 7))
        shared = sb("shared", [P, 4096])
        wv_in = shared[:].rearrange("p (e h) -> p e h", e=E)
        half = NS * D
        xg = shared[:, 0:half].bitcast(F16).rearrange("p (s c) -> p s c", s=NS)
        y_sb = shared[:, half:2 * half].rearrange("p (s d) -> p s d", s=NS)
        wv = sb("wv", [P, 2, E, 2 * H], F16)
        wo_in = sb("wo_in", [P, E, HB * D])
        wo = sb("wo", [P, 2, E, HB * D], F16)
        pT = sb("pT", [P, 2, 2, T], F16)
        fused = sb("fused", [P, 2, 2 * D], F16)
        fused_mid = sb("fused_mid", [P, 2 * D], F16)
        mid = sb("mid", [P, 1])
        mid_k = sb("mid_k", [P, 1])
        owT = sb("owT", [P, 2, D], F16)
        rw_in = sb("rw_in", [P, E])
        rw = sb("rw", [P, 2, E], F16)
        rb = sb("rb", [P, E])
        bias = sb("bias", [P, D])

        ident = sb("ident", [P, P])
        ident16 = sb("ident16", [P, P], F16)
        upper = sb("upper", [P, P], F16)
        below = sb("below", [P, P], F16)
        slot_i = sb("slot_i", [P, CAP], I32)
        slot_row = sb("slot_row", [P, CAP], F16)
        slot_col_i = sb("slot_col_i", [P, NS], I32)
        slot_col = sb("slot_col", [P, NS])
        slot_next = sb("slot_next", [P, NS])
        slot_dump = sb("slot_dump", [P, NS])
        rank_i = sb("rank_i", [P, E], I32)
        rank = sb("rank", [P, E])
        tile_i = sb("tile_i", [P, 1], I32)

        stats = sb("stats", [P, NT, 6])
        mv = sb("mv", [P, NT, 2])
        std = sb("std", [P, NT])
        rstd = sb("rstd", [P, NT])

        logits, rest, first, second, ta = (sb(name, [P, NT, E]) for name in ("logits", "rest", "first", "second", "ta"))
        top1 = sb("top1", [P, NT])
        top2 = sb("top2", [P, NT])
        pick = sb("pick", [P, NT])
        gap = sb("gap", [P, NT])
        egap = sb("egap", [P, NT])
        gate1 = sb("gate1", [P, NT])
        gate2 = sb("gate2", [P, NT])
        mask = sb("mask", [P, E, NT], F16)
        gates = sb("gates", [P, E, NT])
        tot = sb("tot", [P, NB], F16)
        start = sb("start", [P, NB])
        end = sb("end", [P, NB])
        before_end = sb("before_end", [P, NB, CAP], F16)
        in_tile = sb("in_tile", [P, NB, CAP], F16)
        own = sb("own", [P, EB, NB, CAP], F16)
        row_src = sb("row_src", [P, NB, RC], F16)
        row_lo = sb("row_lo", [P, NB, P], F16)
        row = sb("row", [P, 4, RC])
        count = sb("count", [P, NS])
        aux = sb("aux", [P, NS, 2])
        slot_w = sb("slot_w", [P, NS])
        slot_ws = sb("slot_ws", [P, NS])
        unused = sb("unused", [P, NS])
        where = sb("where", [P, NS])
        to_row = sb("to_row", [P, NS], I32)
        from_row = sb("from_row", [P, NS], I32)

        neg_max = sb("neg_max", [P, 4])
        row_sum = sb("row_sum", [P, 4])
        inv_sum = sb("inv_sum", [P, 4])

        xT_flat = xT[:].rearrange("p s n -> p (s n)")
        assert 14 * HB * CAP <= 2 * N

        def after_xT(k, size, dt=F16):
            return xT_flat[:, k * HB * CAP:k * HB * CAP + size].bitcast(dt) if dt != F16 else \
                xT_flat[:, k * HB * CAP:k * HB * CAP + size]

        HC = HB * CAP
        xgT = after_xT(0, 4 * CAP).rearrange("p (q s c) -> p q s c", q=2, s=2)
        hidT = after_xT(2, 4 * HC).rearrange("p (q s c) -> p q s c", q=2, s=2)
        hid = after_xT(6, 4 * HC, F32).rearrange("p (q c) -> p q c", q=2)
        silu = after_xT(10, 2 * HC, F32)
        tanh_b = after_xT(12, 2 * HC, F32)

        x_in = [sem(f"x_in{b}") for b in range(B)]
        small_in, rows_in, w_in_s, wo_in_s = sem("small_in"), sem("rows_in"), sem("w_in"), sem("wo_in")
        zeroed, consts_i, consts = sem("zeroed"), sem("consts_i"), sem("consts")
        stat_s, var_s, std_s, rstd_s, xn_s = sem("stat"), sem("var"), sem("std"), sem("rstd"), sem("xn")
        x_hi, x_lo = sem("x_hi"), sem("x_lo")
        xb_s, xb_out, xg_out = sem("xb"), sem("xb_out"), sem("xg_out")
        mid_s, small_hi, small_lo, band_lo = sem("mid"), sem("small_hi"), sem("small_lo"), sem("band_lo")
        wT_ps, wT_s, fused_ps, fused_s = sem("wT_ps"), sem("wT"), sem("fused_ps"), sem("fused")
        k_s = sem("k")
        wv_hi, wv_lo, wo_hi, wo_lo, w_up = sem("wv_hi"), sem("wv_lo"), sem("wo_hi"), sem("wo_lo"), sem("w_up")
        xT_ps, xT_s = sem("xT_ps"), sem("xT")
        scores_r = sem("router_scores")
        route = sem("route")
        gap_s, egap_s, plan_in = sem("gap"), sem("egap"), sem("plan_in")
        counts_ps, gates_ps = sem("counts_ps"), sem("gates_ps")
        row_hi, row_counts, row_lo_s, tot_s, plan_s = (sem("row_hi"), sem("row_counts"), sem("row_lo"), sem("tot"),
                                                       sem("plan"))
        unit_ps, unit_hi, unit_lo = sem("unit_ps"), sem("unit_hi"), sem("unit_lo")
        s_ready, max_done, exp_done = sem("s_ready"), sem("max_done"), sem("exp_done")
        pt_ready, hi_done, lo_done = sem("pt_ready"), sem("hi_done"), sem("lo_done")
        pv_done, inv_done, o_done = sem("pv_done"), sem("inv_done"), sem("o_done")
        row_ps, row_sb, row_used, list_step, weights_s = (sem("row_ps"), sem("row_sb"), sem("row_used"), sem("list_step"),
                                                      sem("slot_weights"))
        gathered = [sem(f"gathered{i}") for i in range(E // 2)]
        pair_in = sem("pair_in")
        tt_ps, xgT_s = sem("tt_ps"), sem("xgT")
        b_ps, tanh_s, silu_s = sem("b_ps"), sem("tanh_b"), sem("silu")
        a_ps, hid_s, hid_hi, hid_lo = sem("a_ps"), sem("hid"), sem("hid_hi"), sem("hid_lo")
        y_ps, y_s, added = sem("y_ps"), sem("y"), sem("added")
        sum_in = [sem(f"sum_in{i}") for i in range(2)]
        final, out_s = sem("final"), sem("out")

        XT_CREDIT, UNIT_CREDIT, PV_CREDIT, O_CREDIT, ROW_CREDIT, USED_CREDIT, Y_CREDIT = 2, 4, 1, 1, 1, 4, 1

        x_t = x.rearrange("b (n p) d -> p (b n) d", p=P)
        out_t = out.rearrange("b (n p) d -> p (b n) d", p=P)
        sum_t = sum_dram.rearrange("(n p) d -> p n d", p=P)
        xg_t = xg_dram.rearrange("(n p) c -> p n c", p=P)

        block = ctx.enter_context(nc.Block())

        @block.sync
        def _(sp):
            for b in range(B):
                sp.dma_start(x_sb[:, b * BT:(b + 1) * BT, :], x_t[:, b * BT:(b + 1) * BT, :]).then_inc(x_in[b], 16)
            sp.dma_start(rb[:], router_b.rearrange("(a e) -> a e", a=1).to_broadcast([P, E])).then_inc(rows_in, 16)
            sp.dma_start(bias[:], out_b.rearrange("(a d) -> a d", a=1).to_broadcast([P, D])).then_inc(rows_in, 16)
            sp.dma_start(wo_in[:].rearrange("p e (c d) -> p e c d", c=HB),
                         w_out.rearrange("e (c p) d -> p e c d", p=P)).then_inc(wo_in_s, 16)
            sp.dma_start(wv_in[:, :, 0:H], w_in.rearrange("e d h -> d e h")).then_inc(w_in_s, 16)
            sp.dma_start(wv_in[:, :, H:2 * H], v_in.rearrange("e d h -> d e h")).then_inc(w_in_s, 16)
            for b in range(B):
                sp.wait_ge(x_lo, 2 * (b + 1))
                sp.dma_start(xg_t[:, b * BT:(b + 1) * BT, :], xhl[:, b * BT:(b + 1) * BT, :]).then_inc(xg_out, 16)
            for b in range(B):
                sp.wait_ge(xb_s, b + 1)
                sp.dma_start(sum_t[:, b * BT:(b + 1) * BT, :], x_sb[:, b * BT:(b + 1) * BT, :]).then_inc(xb_out, 16)
            sp.dma_start(sum_t[:, NT:NT + CB, :], x_sb[:, 0:CB, :]).then_inc(xb_out, 16)
            sp.wait_ge(added, 16 * NS)
            m = (ITS - 1) * STEPS
            sp.dma_start(x_sb[:, 0:m, :], sum_t[:, 0:m, :]).then_inc(sum_in[0], 16)
            sp.dma_start(x_sb[:, m:NT, :], sum_t[:, m:NT, :]).then_inc(sum_in[1], 16)
            for it in range(ITS - 1):
                t = it * STEPS
                sp.wait_ge(final, it + 1)
                sp.dma_start(out_t[:, t:t + STEPS, :], attn[:, t:t + STEPS, :]).then_inc(out_s, 16)
            for s in range(STEPS):
                t = m + s
                sp.wait_ge(o_done, t + 1 + O_CREDIT)
                sp.dma_start(out_t[:, t, :], attn[:, t, :]).then_inc(out_s, 16)
            sp.wait_ge(out_s, 16 * (ITS - 1 + STEPS))
            sp.wait_ge(xg_out, 16 * B)

        @block.scalar
        def _(act):
            act.dma_start(qkv_in, w_qkv).then_inc(small_in, 16)
            act.dma_start(owT_in, out_wT).then_inc(small_in, 16)
            act.dma_start(rw_in[:], router_wT).then_inc(small_in, 16)
            act.preload_act_table(ACT.Sqrt)

            def std_of(b):
                act.wait_ge(var_s, b + 1)
                act.activation(std[:, b * BT:(b + 1) * BT], mv[:, b * BT:(b + 1) * BT, 1], ACT.Sqrt).then_inc(std_s, 1)

            def x_high(b):
                for h in range(2):
                    t = b * BT + h * G
                    act.wait_ge(xn_s, b + 1)
                    act.activation(xhl[:, t:t + G, 0:D], probs[:, b % 2, h * GC:(h + 1) * GC].rearrange(
                        "p (n d) -> p n d", n=G), ACT.Copy).then_inc(x_hi, 1)

            def turned(b):
                for h in range(2):
                    g = 2 * b + h
                    act.wait_ge(xT_ps, g + 1)
                    act.activation(xT[:, :, g * GC:(g + 1) * GC], psT[:, h, :].bitcast(F16).rearrange(
                        "p (s c) -> p s c", s=2), ACT.Copy).then_inc(xT_s, 1)

            def unit_high(b):
                for h in range(2):
                    g = 2 * b + h
                    act.wait_ge(unit_ps, 2 * g + 1)
                    act.activation(qT[:, HI, g * GC:(g + 1) * GC], psS[:, h, 0, :], ACT.Copy, scale=Q_EVAC).then_inc(unit_hi, 1)
                    act.wait_ge(unit_ps, 2 * g + 2)
                    act.activation(vp[:, g * G:(g + 1) * G, HI, :], psS[:, h, 1, :].rearrange("p (n d) -> p n d", n=G),
                                   ACT.Copy, scale=V_EVAC).then_inc(unit_hi, 1)

            std_of(0)
            act.wait_ge(small_in, 48)
            act.activation(w_hl[:, HI, :], qkv_in, ACT.Copy, scale=W_SCALE).then_inc(small_hi, 1)
            act.activation(owT[:, HI, :], owT_in, ACT.Copy, scale=W_SCALE).then_inc(small_hi, 1)
            act.activation(rw[:, HI, :], rw_in[:], ACT.Copy, scale=W_SCALE).then_inc(small_hi, 1)
            x_high(0)
            act.wait_ge(wT_ps, 1)
            act.activation(wT, psS[:, 0, 0, 0:3 * D].bitcast(F16).rearrange("p (s c) -> p s c", s=2), ACT.Copy).then_inc(wT_s, 1)
            std_of(1)
            turned(0)
            act.wait_ge(fused_ps, 1)
            act.activation(fused[:, HI, :], psO[:, 0:2 * D], ACT.Copy, scale=1.0 / W_SCALE).then_inc(fused_s, 1)
            x_high(1)
            std_of(2)
            turned(1)
            x_high(2)
            std_of(3)
            unit_high(0)
            x_high(3)
            turned(2)
            unit_high(1)
            turned(3)
            unit_high(2)
            unit_high(3)
            act.preload_act_table(ACT.Exp)

            def expert_weights_high(c):
                ce = slice(2 * c, 2 * c + 2)
                act.activation(wv[:, HI, ce, :], wv_in[:, ce, :], ACT.Copy, scale=W_SCALE).then_inc(wv_hi, 1)

            act.wait_ge(w_in_s, 32)
            expert_weights_high(0)
            expert_weights_high(1)
            act.wait_ge(gap_s, 1)
            act.activation(egap[:], gap[:], ACT.Exp).then_inc(egap_s, 1)
            expert_weights_high(2)
            expert_weights_high(3)

            def exp_of(i, par):
                act.wait_ge(max_done, i + 1)
                act.activation(probs[:, par % 2, :], psS[:, par % 2].rearrange("p a c -> p (a c)"), ACT.Exp,
                               bias=neg_max[:, par % 4:par % 4 + 1],
                               accum_out=row_sum[:, par % 4:par % 4 + 1]).then_inc(exp_done, 1)

            def probs_high(i, par):
                for h in range(2):
                    act.wait_ge(pt_ready, 2 * i + h + 1)
                    if h == 0:
                        act.wait_ge(pv_done, i - 1 + PV_CREDIT)
                    act.activation(pT[:, par % 2, HI, h * 512:(h + 1) * 512], psT[:, h, :], ACT.Copy).then_inc(hi_done, 1)

            def scale_out(i, par):
                act.wait_ge(inv_done, i + 1)
                act.wait_ge(pv_done, i + 1 + PV_CREDIT)
                act.activation(attn[:, bass.ds(i, 1), :].rearrange("p a d -> p (a d)"), psO[:, 0:D], ACT.Copy,
                               scale=inv_sum[:, par % 4:par % 4 + 1]).then_inc(o_done, 1)

            def row_out(e, s, j):
                u = 2 * e + j
                act.wait_ge(row_ps, u + 1)
                act.wait_ge(row_used, u + 1 - 4 + USED_CREDIT)
                act.activation(row[:, (2 * s + j) % 4, :], psM[:, 0:RC], ACT.Copy).then_inc(row_sb, 1)

            def tanh_of(e):
                act.wait_ge(b_ps, e + 1)
                act.activation(tanh_b, psM[:], ACT.Tanh, scale=0.5 / W_SCALE).then_inc(tanh_s, 1)

            def hid_high(e, q):
                act.wait_ge(hid_s, e + 1)
                act.activation(hidT[:, q, HI, :], hid[:, q, :], ACT.Copy).then_inc(hid_hi, 1)

            def y_out(e):
                act.wait_ge(y_ps, e + 1)
                for j in range(CB):
                    ins = act.activation(y_sb[:, bass.ds(2 * e + j, 1), :].rearrange("p a d -> p (a d)"),
                                         psM[:, j * D:(j + 1) * D], ACT.Copy,
                                         scale=slot_ws[:, bass.ds(2 * e + j, 1)])
                ins.then_inc(y_s, 1)

            def steps(it, lists=False, experts=False, last=False):
                for s in range(STEPS):
                    i = it * STEPS + s
                    e0 = 2 * (it - 2)
                    if lists:
                        row_out(4 * it + s, s, 0)
                    if experts and s in (2, 3):
                        hid_high(e0 + s - 2, s - 2)
                    if experts and s in (1, 2):
                        tanh_of(e0 + s - 1)
                    if not last or s < STEPS - 1:
                        probs_high(i + 1, s + 1)
                    if experts and s == 3:
                        y_out(e0)
                    if lists:
                        row_out(4 * it + s, s, 1)
                    if not last or s < STEPS - 2:
                        exp_of(i + 2, s + 2)
                    if lists:
                        scale_out(i, s)
                    if experts and s == 3:
                        y_out(e0 + 1)

            exp_of(0, 0)
            exp_of(1, 1)
            for h in range(2):
                act.wait_ge(pt_ready, h + 1)
                act.activation(pT[:, 0, HI, h * 512:(h + 1) * 512], psT[:, h, :], ACT.Copy).then_inc(hi_done, 1)
            act.wait_ge(gates_ps, 1)
            act.activation(row_src[:, :, P:2 * P], psM[:, NB * P:2 * NB * P].rearrange("p (h t) -> p h t", h=NB),
                           ACT.Copy).then_inc(row_hi, 1)
            act.activation(row_src[:, :, 0:P], psM[:, 0:NB * P].rearrange("p (h t) -> p h t", h=NB),
                           ACT.Copy).then_inc(row_counts, 1)
            with act.Fori(0, 2) as it:
                steps(it, lists=True)
            act.wait_ge(weights_s, 2)
            with act.Fori(2, 6) as it:
                steps(it, experts=True)
            steps(6)
            steps(7, last=True)

        @block.vector
        def _(dve):
            dve.memset(mid[:], 0.0).then_inc(mid_s, 1)
            dve.memset(mid_k[:], 0.0).then_inc(mid_s, 1)
            dve.memset(neg_max[:], 0.0).then_inc(xT_s, XT_CREDIT)
            dve.memset(row_sum[:], 0.0).then_inc(unit_lo, UNIT_CREDIT)
            dve.memset(inv_sum[:], 0.0).then_inc(pv_done, PV_CREDIT)
            dve.memset(count[:], 0.0).then_inc(o_done, O_CREDIT)
            dve.memset(aux[:], 0.0).then_inc(row_sb, ROW_CREDIT)
            dve.memset(slot_w[:], 0.0).then_inc(row_used, USED_CREDIT)
            dve.memset(unused[:], 0.0).then_inc(y_s, Y_CREDIT)
            dve.wait_ge(mid_s, 2)
            for m0 in (LOW, 2 * LOW):
                dve.memset(mid[m0:m0 + LOW], 1.0).then_inc(mid_s, 1)
                dve.memset(mid_k[m0:m0 + LOW], K_SCALE).then_inc(mid_s, 1)

            def stats_of(b):
                dve.wait_ge(x_in[b], 16)
                for t in range(b * BT, (b + 1) * BT):
                    ins = dve.bn_stats(stats[:, t, :], x_sb[:, t, :])
                ins.then_inc(stat_s, 1)
                dve.wait_ge(stat_s, 2 * b + 1)
                for t in range(b * BT, (b + 1) * BT):
                    ins = dve.bn_aggr(mv[:, t, :], stats[:, t, :])
                ins.then_inc(stat_s, 1)
                dve.wait_ge(stat_s, 2 * b + 2)
                v = mv[:, b * BT:(b + 1) * BT, 1]
                dve.tensor_scalar(v, v, EPS, None, ALU.add).then_inc(var_s, 1)

            def normalise(b):
                dve.wait_ge(std_s, b + 1)
                dve.reciprocal(rstd[:, b * BT:(b + 1) * BT], std[:, b * BT:(b + 1) * BT]).then_inc(rstd_s, 1)
                dve.wait_ge(rstd_s, b + 1)
                if b >= 2:
                    dve.wait_ge(x_lo, 2 * (b - 1))
                for k in range(BT):
                    t = b * BT + k
                    ins = dve.tensor_scalar(probs[:, b % 2, k * D:(k + 1) * D], x_sb[:, t, :], mv[:, t, 0:1],
                                            rstd[:, t:t + 1], ALU.subtract, ALU.mult)
                ins.then_inc(xn_s, 1)

            def unit_low(b, halves=(0, 1)):
                for h in halves:
                    g = 2 * b + h
                    at = slice(g * GC, (g + 1) * GC)
                    dve.wait_ge(unit_hi, 2 * g + 1)
                    dve.scalar_tensor_tensor(out=qT[:, LO, at], in0=psS[:, h, 0, :], scalar=Q_EVAC, in1=qT[:, HI, at],
                                             op0=ALU.mult, op1=ALU.subtract).then_inc(unit_lo, 1)
                    at = slice(g * G, (g + 1) * G)
                    dve.wait_ge(unit_hi, 2 * g + 2)
                    dve.scalar_tensor_tensor(out=vp[:, at, LO, :], in0=psS[:, h, 1, :].rearrange("p (n d) -> p n d", n=G),
                                             scalar=V_EVAC, in1=vp[:, at, HI, :], op0=ALU.mult,
                                             op1=ALU.subtract).then_inc(unit_lo, 1)

            dve.wait_ge(consts_i, 4)
            dve.tensor_copy(slot_row[:], slot_i[:])
            dve.tensor_copy(slot_col[:], slot_col_i[:])
            dve.tensor_scalar(slot_next[:], slot_col_i[:], 1.0, None, ALU.add)
            dve.tensor_scalar(slot_dump[:], slot_col_i[:], float(N - P), None, ALU.add)
            dve.tensor_copy(rank[:], rank_i[:])
            for h in range(NB):
                dve.memset(row_src[:, h, 2 * P + 1:RC], 1.0)
                for e in range(EB):
                    rows = slice(e * NT, (e + 1) * NT)
                    ins = dve.tensor_scalar(row_src[rows, h, 2 * P:2 * P + 1], tile_i[rows], float(-e * N), None, ALU.add)
            ins.then_inc(consts, 1)
            stats_of(0)
            normalise(0)
            dve.wait_ge(small_hi, 3)
            for w_in_f32, hi, lo in ((qkv_in, w_hl[:, HI, :], w_hl[:, LO, :]), (owT_in, owT[:, HI, :], owT[:, LO, :]),
                                     (rw_in[:], rw[:, HI, :], rw[:, LO, :])):
                dve.scalar_tensor_tensor(out=lo, in0=w_in_f32, scalar=W_SCALE, in1=hi, op0=ALU.mult,
                                         op1=ALU.subtract).then_inc(small_lo, 1)
            dve.wait_ge(mid_s, 6)
            dve.wait_ge(small_lo, 3)
            dve.tensor_scalar(w_hl[:, LO, :], w_hl[:, LO, :], mid[:, 0:1], None, ALU.mult).then_inc(band_lo, 1)
            stats_of(1)
            normalise(1)
            dve.wait_ge(fused_s, 1)
            dve.scalar_tensor_tensor(out=fused[:, LO, :], in0=psO[:, 0:2 * D], scalar=1.0 / W_SCALE, in1=fused[:, HI, :],
                                     op0=ALU.mult, op1=ALU.subtract).then_inc(fused_s, 1)
            dve.tensor_scalar(fused_mid[:], fused[:, HI, :], mid[:, 0:1], None, ALU.mult).then_inc(fused_s, 1)
            stats_of(2)
            normalise(2)
            stats_of(3)
            normalise(3)
            unit_low(0)
            unit_low(1)
            unit_low(2)

            def max_of(i, par):
                dve.wait_ge(s_ready, i + 1)
                dve.tensor_reduce(neg_max[:, par % 4:par % 4 + 1], psS[:, par % 2].rearrange("p a c -> p (a c)"),
                                  AX, ALU.max, negate=True).then_inc(max_done, 1)

            def probs_low(i, par):
                for h in range(2):
                    cols = slice(h * 512, (h + 1) * 512)
                    dve.wait_ge(hi_done, 2 * i + h + 1)
                    dve.tensor_tensor(pT[:, par % 2, LO, cols], psT[:, h, :], pT[:, par % 2, HI, cols],
                                      ALU.subtract).then_inc(lo_done, 1)

            n = [0]

            def then(ins):
                n[0] += 1
                ins.then_inc(route, 1)
                dve.wait_ge(route, n[0])

            def over_e(a):
                return a[:].unsqueeze(2).to_broadcast([P, NT, E])

            rank_b = rank[:].unsqueeze(1).to_broadcast([P, NT, E])
            rb_b = rb[:].unsqueeze(1).to_broadcast([P, NT, E])
            dve.wait_ge(scores_r, NG)
            dve.wait_ge(rows_in, 32)
            dve.wait_ge(consts, 1)
            then(dve.scalar_tensor_tensor(out=logits[:], in0=psM[:, 0:NT * E].rearrange("p (n e) -> p n e", e=E),
                                          scalar=1.0 / W_SCALE, in1=rb_b, op0=ALU.mult, op1=ALU.add))
            then(dve.tensor_reduce(top1[:], logits[:], AX, ALU.max))
            then(dve.tensor_tensor(ta[:], logits[:], over_e(top1), ALU.is_equal))
            unit_low(3, (0,))
            then(dve.tensor_tensor(ta[:], ta[:], rank_b, ALU.mult))
            then(dve.tensor_reduce(pick[:], ta[:], AX, ALU.max))
            then(dve.tensor_tensor(first[:], rank_b, over_e(pick), ALU.is_equal))
            then(dve.scalar_tensor_tensor(out=rest[:], in0=first[:], scalar=-BIG, in1=logits[:], op0=ALU.mult, op1=ALU.add))
            unit_low(3, (1,))
            max_of(0, 0)
            then(dve.tensor_reduce(top2[:], rest[:], AX, ALU.max))
            dve.tensor_tensor(gap[:], top2[:], top1[:], ALU.subtract).then_inc(gap_s, 1)
            then(dve.tensor_tensor(ta[:], rest[:], over_e(top2), ALU.is_equal))
            then(dve.tensor_tensor(ta[:], ta[:], rank_b, ALU.mult))
            then(dve.tensor_reduce(pick[:], ta[:], AX, ALU.max))
            then(dve.tensor_tensor(second[:], rank_b, over_e(pick), ALU.is_equal))
            dve.tensor_tensor(mask[:].rearrange("p e n -> p n e"), first[:], second[:], ALU.add).then_inc(plan_in, 1)
            dve.wait_ge(egap_s, 1)
            then(dve.tensor_scalar(pick[:], egap[:], 1.0, None, ALU.add))
            then(dve.reciprocal(gate1[:], pick[:]))
            max_of(1, 1)
            dve.wait_ge(counts_ps, 1)
            counts = psM[:, 0:NB * P].rearrange("p (h t) -> p h t", h=NB)
            dve.tensor_copy(tot[:], counts[:, :, P - 1]).then_inc(tot_s, 1)
            then(dve.tensor_tensor(gate2[:], gate1[:], egap[:], ALU.mult))
            dve.tensor_tensor(first[:], first[:], over_e(gate1), ALU.mult)
            then(dve.tensor_tensor(second[:], second[:], over_e(gate2), ALU.mult))
            dve.tensor_tensor(gates[:].rearrange("p e n -> p n e"), first[:], second[:], ALU.add).then_inc(plan_in, 1)
            probs_low(0, 0)
            dve.wait_ge(row_counts, 1)
            dve.tensor_tensor(row_lo[:], psM[:, NB * P:2 * NB * P].rearrange("p (h t) -> p h t", h=NB),
                              row_src[:, :, P:2 * P], ALU.subtract).then_inc(row_lo_s, 1)
            then(dve.tensor_copy(end[:], counts[:, :, P - 1]))
            then(dve.tensor_tensor(start[:], end[:], tot[:], ALU.subtract))
            for h in range(NB):
                ins = dve.tensor_scalar(before_end[:, h, :], slot_row[:], end[:, h:h + 1], None, ALU.is_lt)
            then(ins)
            for h in range(NB):
                ins = dve.scalar_tensor_tensor(out=in_tile[:, h, :], in0=slot_row[:], scalar=start[:, h:h + 1],
                                               in1=before_end[:, h, :], op0=ALU.is_ge, op1=ALU.mult)
            then(ins)
            dve.wait_ge(zeroed, 5)
            for e in range(EB):
                rows = slice(e * NT, (e + 1) * NT)
                ins = dve.tensor_copy(own[rows, e, :, :], in_tile[rows])
            ins.then_inc(plan_s, 1)

            def invert_sum(i, par):
                c = slice(par % 4, par % 4 + 1)
                dve.wait_ge(exp_done, i + 1)
                dve.reciprocal(inv_sum[:, c], row_sum[:, c]).then_inc(inv_done, 1)

            def scale_out(i, par, last):
                c = slice(par % 4, par % 4 + 1)
                dve.wait_ge(inv_done, i + 1)
                dve.wait_ge(pv_done, i + 1 + PV_CREDIT)
                if last:
                    dve.wait_ge(sum_in[1], 16)
                    dve.scalar_tensor_tensor(out=attn[:, i, :], in0=psO[:, 0:D], scalar=inv_sum[:, c],
                                             in1=x_sb[:, i, :], op0=ALU.mult, op1=ALU.add).then_inc(o_done, 1)
                else:
                    dve.tensor_scalar(attn[:, bass.ds(i, 1), :].rearrange("p a d -> p (a d)"), psO[:, 0:D],
                                      inv_sum[:, c], None, ALU.mult).then_inc(o_done, 1)

            def row_read(e, s, j):
                u = 2 * e + j
                r = row[:, (2 * s + j) % 4, :]
                dve.wait_ge(row_sb, u + 1 + ROW_CREDIT)
                dve.scalar_tensor_tensor(out=r[:, P:2 * P], in0=r[:, 0:P], scalar=slot_next[:, j:j + 1],
                                         in1=r[:, P:2 * P], op0=ALU.is_equal, op1=ALU.mult,
                                         accum_out=slot_w[:, bass.ds(u, 1)])
                dve.tensor_scalar(r[:, 0:P], r[:, 0:P], slot_col[:, j:j + 1], None, ALU.is_le, ALU.add,
                                  accum_out=count[:, bass.ds(u, 1)])
                dve.tensor_copy(aux[:, bass.ds(u, 1), :].rearrange("p a c -> p (a c)"), r[:, 2 * P:RC]).then_inc(row_used, 1)

            def gate_of(e):
                dve.wait_ge(tanh_s, e + 1)
                dve.scalar_tensor_tensor(out=silu, in0=tanh_b, scalar=1.0, in1=psM[:], op0=ALU.add,
                                         op1=ALU.mult).then_inc(silu_s, 1)

            def hidden_of(e, q):
                dve.wait_ge(a_ps, e + 1)
                dve.wait_ge(silu_s, e + 1)
                dve.scalar_tensor_tensor(out=hid[:, q, :], in0=psM[:], scalar=0.5 / (W_SCALE * W_SCALE), in1=silu,
                                         op0=ALU.mult, op1=ALU.mult).then_inc(hid_s, 1)

            def steps(it, lists=False, experts=False, last=False):
                for s in range(STEPS):
                    i = it * STEPS + s
                    e0 = 2 * (it - 2)
                    if experts and s in (2, 3):
                        hidden_of(e0 + s - 2, s - 2)
                    if not last or s < STEPS - 2:
                        max_of(i + 2, s + 2)
                    if experts and s in (1, 2):
                        gate_of(e0 + s - 1)
                    if not last or s < STEPS - 1:
                        probs_low(i + 1, s + 1)
                    if lists:
                        row_read(4 * it + s, s, 0)
                    if lists:
                        row_read(4 * it + s, s, 1)
                    invert_sum(i, s)
                    if not lists:
                        scale_out(i, s, last)
                    if experts and s == 0:
                        dve.wait_ge(tt_ps, it - 2 + 1)
                        dve.tensor_copy(xgT, psM[:].bitcast(F16).rearrange("p (q s c) -> p q s c", q=2, s=2)).then_inc(xgT_s, 1)

            with dve.Fori(0, 2) as it:
                steps(it, lists=True)
            with dve.Fori(2, 6) as it:
                steps(it, experts=True)
            steps(6)
            steps(7, last=True)

        @block.gpsimd
        def _(pool):
            pool.iota(slot_i[:], [[1, CAP]], base=0, channel_multiplier=0).then_inc(consts_i, 1)
            pool.iota(slot_col_i[:].rearrange("p (e j) -> p e j", j=CB), [[0, E], [P, CB]], base=0,
                      channel_multiplier=1).then_inc(consts_i, 1)
            pool.iota(rank_i[:], [[-1, E]], base=E, channel_multiplier=0).then_inc(consts_i, 1)
            pool.iota(tile_i[:], [[0, 1]], base=0, channel_multiplier=P).then_inc(consts_i, 1)
            pool.memset(ident16[:], 0.0).then_inc(zeroed, 1)
            pool.memset(ident[:], 0.0).then_inc(zeroed, 1)
            pool.memset(upper[:], 1.0).then_inc(zeroed, 1)
            pool.memset(below[:], 1.0).then_inc(zeroed, 1)
            pool.wait_ge(zeroed, 4)
            for t in (ident16, ident):
                pool.affine_select(out=t[:], in_=t[:], compare_op=ALU.not_equal, fill=1.0, base=0, pattern=[[-1, P]],
                                   channel_multiplier=1).then_inc(consts_i, 1)
            pool.affine_select(out=upper[:], in_=upper[:], compare_op=ALU.is_ge, fill=0.0, base=0, pattern=[[1, P]],
                               channel_multiplier=-1).then_inc(consts_i, 1)
            pool.affine_select(out=below[:], in_=below[:], compare_op=ALU.is_gt, fill=0.0, base=0, pattern=[[1, P]],
                               channel_multiplier=-1).then_inc(consts_i, 1)
            pool.wait_ge(consts_i, 8)
            for e in range(1, EB):
                pool.memset(below[0:e * NT, e * NT:(e + 1) * NT], 0.0).then_inc(consts_i, 1)
            pool.memset(own[:], 0.0).then_inc(zeroed, 1)
            def keys(b):
                at = slice(b * T, (b + 1) * T)
                pool.wait_ge(xT_s, 2 * (b + 1) + XT_CREDIT)
                pool.tensor_scalar(kT[:, HI, at], xT[:, HI, at], K_SCALE, 0.0, ALU.mult, ALU.add).then_inc(k_s, 1)
                pool.tensor_scalar(kT[:, LO, at], xT[:, LO, at], mid_k[:, 0:1], 0.0, ALU.mult, ALU.add).then_inc(k_s, 1)

            pool.wait_ge(mid_s, 6)
            for b in range(B):
                for h in range(2):
                    t = b * BT + h * G
                    pool.wait_ge(x_hi, 2 * b + h + 1)
                    pool.tensor_tensor(xhl[:, t:t + G, D:2 * D], probs[:, b % 2, h * GC:(h + 1) * GC].rearrange(
                        "p (n d) -> p n d", n=G), xhl[:, t:t + G, 0:D], ALU.subtract).then_inc(x_lo, 1)
            for b in range(B):
                keys(b)
            pool.wait_ge(rows_in, 32)
            bias_b = bias[:].unsqueeze(1).to_broadcast([P, BT, D])
            for b in range(B):
                xb = x_sb[:, b * BT:(b + 1) * BT, :]
                pool.tensor_tensor(xb, xb, bias_b, ALU.add).then_inc(xb_s, 1)
            pool.wait_ge(wo_in_s, 16)
            pool.tensor_scalar(wo_in[:], wo_in[:], W_SCALE, 0.0, ALU.mult, ALU.add).then_inc(w_up, 1)
            pool.wait_ge(w_up, 1)
            pool.tensor_scalar(wo[:, HI], wo_in[:], 1.0, 0.0, ALU.mult, ALU.add).then_inc(wo_hi, 1)
            pool.wait_ge(wo_hi, 1)
            pool.tensor_tensor(wo[:, LO], wo_in[:], wo[:, HI], ALU.subtract).then_inc(wo_lo, 1)
            pool.wait_ge(w_in_s, 32)
            for c in range(4):
                ce = slice(2 * c, 2 * c + 2)
                pool.wait_ge(wv_hi, c + 1)
                pool.tensor_scalar(wv_in[:, ce, :], wv_in[:, ce, :], W_SCALE, 0.0, ALU.mult, ALU.add).then_inc(w_up, 1)
                pool.wait_ge(w_up, c + 2)
                pool.tensor_tensor(wv[:, LO, ce, :], wv_in[:, ce, :], wv[:, HI, ce, :], ALU.subtract).then_inc(wv_lo, 1)
            def slot_lists(c):
                k = slice(c * (NS // 2), (c + 1) * (NS // 2))
                n = 6 * c
                pool.wait_ge(row_used, (c + 1) * (NS // 2) + USED_CREDIT)
                pool.tensor_scalar(slot_ws[:, k], slot_w[:, k], 1.0 / W_SCALE, None, ALU.mult).then_inc(weights_s, 1)
                pool.tensor_scalar(unused[:, k], aux[:, k, 1], -1.0, 1.0, ALU.mult, ALU.add).then_inc(list_step, 1)
                pool.tensor_tensor(where[:, k], aux[:, k, 0], count[:, k], ALU.add).then_inc(list_step, 1)
                pool.wait_ge(list_step, n + 2)
                pool.tensor_tensor(unused[:, k], unused[:, k], slot_dump[:, k], ALU.mult).then_inc(list_step, 1)
                pool.wait_ge(list_step, n + 3)
                pool.tensor_tensor(where[:, k], where[:, k], unused[:, k], ALU.add).then_inc(list_step, 1)
                pool.wait_ge(list_step, n + 4)
                pool.tensor_scalar(from_row[:, k], where[:, k], float(N - 1), None, ALU.min).then_inc(list_step, 1)
                pool.tensor_copy(to_row[:, k], where[:, k]).then_inc(list_step, 1)
                pool.wait_ge(list_step, n + 6)

            pool.wait_ge(xg_out, 16 * B)
            pool.wait_ge(wv_lo, 4)
            for k in range(NS):
                if k % (NS // 2) == 0:
                    slot_lists(k // (NS // 2))
                pool.indirect_dma_start(xg[:, k, :], None, xg_dram[:, :],
                                        bass.IndirectOffsetOnAxis(ap=from_row[:, k:k + 1], axis=0),
                                        bounds_check=N - 1, oob_is_err=True).then_inc(gathered[k // 4], 16)
            for i in range(E // 2):
                pool.wait_ge(gathered[i], 64)
                pool.sem_inc(pair_in, 1)
            pool.wait_ge(xb_out, 16 * (B + 1))
            for e in range(E):
                pool.wait_ge(hid_s, e + 1)
                pool.wait_ge(hid_hi, e + 1)
                pool.tensor_tensor(hidT[:, e % 2, LO, :], hid[:, e % 2, :], hidT[:, e % 2, HI, :],
                                   ALU.subtract).then_inc(hid_lo, 1)
                if e % 2 == 0:
                    continue
                for ee in (e - 1, e):
                    pool.wait_ge(y_s, ee + 1 + Y_CREDIT)
                    if ee > 0:
                        pool.wait_ge(added, 16 * CB * ee)
                    for j in range(CB):
                        k = ee * CB + j
                        pool.indirect_dma_start(sum_dram[:, :], bass.IndirectOffsetOnAxis(ap=to_row[:, k:k + 1], axis=0),
                                                y_sb[:, k, :], None, bounds_check=N + CAP - 1, oob_is_err=True,
                                                compute_op=ALU.add).then_inc(added, 16)
            pool.wait_ge(sum_in[0], 16)
            for it in range(ITS - 1):
                t = slice(it * STEPS, (it + 1) * STEPS)
                pool.wait_ge(o_done, (it + 1) * STEPS + O_CREDIT)
                pool.tensor_tensor(attn[:, t, :], attn[:, t, :], x_sb[:, t, :], ALU.add).then_inc(final, 1)

        @block.tensor
        def _(pe):
            def mm(o, a, b, first, last):
                return pe.matmul(o, a, b, start=first, stop=last)

            pe.wait_ge(consts_i, 8 + EB - 1)
            pe.wait_ge(small_lo, 3)
            pe.wait_ge(band_lo, 1)
            bank = psS[:, 0, 0, 0:3 * D].bitcast(F16)
            for s in (HI, LO):
                for w in range(3):
                    ins = pe.transpose(bank[:, (3 * s + w) * D:(3 * s + w + 1) * D], w_hl[:, s, w * D:(w + 1) * D], ident16[:])
            ins.then_inc(wT_ps, 1)
            def turn(b):
                for h in range(2):
                    g = 2 * b + h
                    pe.wait_ge(x_lo, g + 1)
                    pe.wait_ge(xT_s, g + 1 - 2 + XT_CREDIT)
                    bank = psT[:, h, :].bitcast(F16)
                    for s in (HI, LO):
                        for t in range(G):
                            ins = pe.transpose(bank[:, (s * G + t) * P:(s * G + t + 1) * P],
                                               xhl[:, g * G + t, s * D:(s + 1) * D],
                                               ident16[:])
                    ins.then_inc(xT_ps, 1)

            turn(0)
            pe.wait_ge(wT_s, 1)
            for c in range(2):
                o = psO[:, c * D:(c + 1) * D]
                (l_hi, r_hi), (l_lo, r_lo) = ((wT[:, s, 0:D], wT[:, s, D:2 * D]) if c == 0 else
                                              (wT[:, s, 2 * D:3 * D], owT[:, s, :]) for s in (HI, LO))
                mm(o, l_hi, r_hi, True, False)
                mm(o, l_hi, r_lo, False, False)
                ins = mm(o, l_lo, r_hi, False, True)
            ins.then_inc(fused_ps, 1)
            for b in range(B):
                if b + 1 < B:
                    turn(b + 1)
                for h in range(2):
                    g = 2 * b + h
                    pe.wait_ge(xT_s, g + 1 + XT_CREDIT)
                    for t in range(G):
                        o = psM[:, (g * G + t) * E:(g * G + t + 1) * E]
                        at = slice((g * G + t) * P, (g * G + t + 1) * P)
                        mm(o, xT[:, HI, at], rw[:, HI, :], True, False)
                        mm(o, xT[:, HI, at], rw[:, LO, :], False, False)
                        ins = mm(o, xT[:, LO, at], rw[:, HI, :], False, True)
                    ins.then_inc(scores_r, 1)
                for h in range(2):
                    g = 2 * b + h
                    pe.wait_ge(fused_s, 3)
                    pe.wait_ge(unit_lo, 2 * g + 1 - 4 + UNIT_CREDIT)
                    o = psS[:, h, 0, :]
                    at = slice(g * GC, (g + 1) * GC)
                    mm(o, fused[:, HI, 0:D], xT[:, HI, at], True, False)
                    mm(o, fused[:, LO, 0:D], xT[:, HI, at], False, False)
                    mm(o, fused_mid[:, 0:D], xT[:, LO, at], False, True).then_inc(unit_ps, 1)
                    pe.wait_ge(unit_lo, 2 * g + 2 - 4 + UNIT_CREDIT)
                    for t in range(G):
                        o = psS[:, h, 1, t * D:(t + 1) * D]
                        at = slice((g * G + t) * P, (g * G + t + 1) * P)
                        mm(o, xT[:, HI, at], fused[:, HI, D:2 * D], True, False)
                        mm(o, xT[:, HI, at], fused[:, LO, D:2 * D], False, False)
                        ins = mm(o, xT[:, LO, at], fused_mid[:, D:2 * D], False, True)
                    ins.then_inc(unit_ps, 1)

            def scores(i, batch, par):
                for c in range(2):
                    o = psS[:, par % 2, c, :]
                    at = bass.ds(i * P, P)
                    key = bass.ds(batch * T + c * 512, 512)
                    mm(o, qT[:, HI, at], kT[:, HI, key], True, False)
                    mm(o, qT[:, HI, at], kT[:, LO, key], False, False)
                    ins = mm(o, qT[:, LO, at], kT[:, HI, key], False, True)
                ins.then_inc(s_ready, 1)

            def turn_probs(i, par, first):
                pe.wait_ge(exp_done, i + 1)
                for h in range(2):
                    if not first:
                        pe.wait_ge(lo_done, 2 * (i - 1) + h + 1)
                    for k in range(4):
                        ins = pe.transpose(psT[:, h, k * P:(k + 1) * P], probs[:, par % 2, (4 * h + k) * P:(4 * h + k + 1) * P],
                                           ident[:])
                    ins.then_inc(pt_ready, 1)

            def weigh_values(i, batch, par):
                pe.wait_ge(lo_done, 2 * i + 2)
                pe.wait_ge(o_done, i + O_CREDIT)
                for k in range(BT):
                    ph, pl = (pT[:, par % 2, s, k * P:(k + 1) * P] for s in (HI, LO))
                    v_hi, v_lo = (vp[:, bass.ds(batch * BT + k, 1), s, :].rearrange("p a d -> p (a d)") for s in (HI, LO))
                    mm(psO[:, 0:D], ph, v_hi, k == 0, False)
                    mm(psO[:, 0:D], ph, v_lo, False, False)
                    ins = mm(psO[:, 0:D], pl, v_hi, False, k == BT - 1)
                ins.then_inc(pv_done, 1)

            def slot_rows(it, s, j):
                pe.wait_ge(plan_s, 1)
                pe.wait_ge(row_sb, 2 * (EB * it + s) + j + ROW_CREDIT)
                h = bass.ds(it, 1)
                a = own[:, s, h, j * P:(j + 1) * P].rearrange("p a c -> p (a c)")
                mm(psM[:, 0:RC], a, row_src[:, h, :].rearrange("p a c -> p (a c)"), True, False)
                mm(psM[:, P:2 * P], a, row_lo[:, h, :].rearrange("p a c -> p (a c)"), False, True).then_inc(row_ps, 1)

            def turn_rows(p):
                pe.wait_ge(pair_in, p + 1)
                pe.wait_ge(y_s, 2 * p + Y_CREDIT)
                bank = psM[:].bitcast(F16)
                for q in range(2):
                    for s in (HI, LO):
                        for j in range(CB):
                            o = ((q * 2 + s) * CB + j) * P
                            ins = pe.transpose(bank[:, o:o + P], xg[:, bass.ds(4 * p + 2 * q + j, 1), s * D:(s + 1) * D]
                                               .rearrange("p a d -> p (a d)"), ident16[:])
                ins.then_inc(tt_ps, 1)

            def branch(e, q, off):
                for c in range(HB):
                    o = psM[:, c * CAP:(c + 1) * CAP]
                    wh, wl = (wv[:, s, bass.ds(e, 1), off + c * P:off + (c + 1) * P].rearrange("p a h -> p (a h)")
                              for s in (HI, LO))
                    mm(o, wh, xgT[:, q, HI, :], True, False)
                    mm(o, wl, xgT[:, q, HI, :], False, False)
                    ins = mm(o, wh, xgT[:, q, LO, :], False, True)
                return ins

            def expert_out(e, q):
                pe.wait_ge(hid_lo, e + 1)
                for j in range(CB):
                    o = psM[:, j * D:(j + 1) * D]
                    for c in range(HB):
                        hh, hl = (hidT[:, q, s, c * CAP + j * P:c * CAP + (j + 1) * P] for s in (HI, LO))
                        w_hi, w_lo = (wo[:, s, bass.ds(e, 1), c * D:(c + 1) * D].rearrange("p a d -> p (a d)")
                                      for s in (HI, LO))
                        mm(o, hh, w_hi, c == 0, False)
                        mm(o, hh, w_lo, False, False)
                        ins = mm(o, hl, w_hi, False, c == HB - 1)
                ins.then_inc(y_ps, 1)

            def steps(it, lists=False, experts=False, last=False):
                for s in range(STEPS):
                    i = it * STEPS + s
                    e0 = 2 * (it - 2)
                    if not last or s < STEPS - 2:
                        pe.wait_ge(exp_done, i + 1)
                        scores(i + 2, (it + s // 2) >> 1, s + 2)
                    if lists:
                        slot_rows(it, s, 0)
                    if experts and s in (1, 2):
                        pe.wait_ge(xgT_s, it - 2 + 1)
                        if s == 2:
                            pe.wait_ge(hid_s, e0 + 1)
                        branch(e0 + s - 1, s - 1, H).then_inc(b_ps, 1)
                    if experts and s == 3:
                        pe.wait_ge(hid_s, e0 + 2)
                        expert_out(e0, 0)
                    if not last or s < STEPS - 1:
                        turn_probs(i + 1, s + 1, False)
                    if lists:
                        slot_rows(it, s, 1)
                    weigh_values(i, it >> 1, s)
                    if experts and s == 0:
                        turn_rows(it - 2)
                    if experts and s in (1, 2):
                        pe.wait_ge(silu_s, e0 + s)
                        branch(e0 + s - 1, s - 1, 0).then_inc(a_ps, 1)
                    if experts and s == 3:
                        pe.wait_ge(y_s, e0 + 1 + Y_CREDIT)
                        expert_out(e0 + 1, 1)

            pe.wait_ge(k_s, 2 * B)
            pe.wait_ge(unit_lo, 4 * B - 2 + UNIT_CREDIT)
            scores(0, 0, 0)
            pe.wait_ge(unit_lo, 4 * B + UNIT_CREDIT)
            scores(1, 0, 1)
            pe.wait_ge(plan_in, 1)
            def counts(h, alone):
                return mm(psM[:, h * P:(h + 1) * P], mask[:, h * EB:(h + 1) * EB, :].rearrange("p e n -> p (e n)"), upper[:],
                          True, alone)

            for h in range(NB):
                ins = counts(h, True)
            ins.then_inc(counts_ps, 1)
            turn_probs(0, 0, True)
            pe.wait_ge(tot_s, 1)
            for h in range(NB):
                counts(h, False)
                mm(psM[:, h * P:(h + 1) * P], below[:], tot[:, h:h + 1].to_broadcast([P, P]), False, True)
            pe.wait_ge(plan_in, 2)
            for h in range(NB):
                ins = pe.transpose(psM[:, (NB + h) * P:(NB + h + 1) * P],
                                   gates[:, h * EB:(h + 1) * EB, :].rearrange("p e n -> p (e n)"), ident[:])
            ins.then_inc(gates_ps, 1)
            with pe.Fori(0, 2) as it:
                steps(it, lists=True)
            pe.wait_ge(row_sb, NS + ROW_CREDIT)
            pe.wait_ge(wo_lo, 1)
            pe.wait_ge(wv_lo, 4)
            with pe.Fori(2, 6) as it:
                steps(it, experts=True)
            steps(6)
            steps(7, last=True)


_INS = ["x", "w_qkv", "out_wT", "out_b", "router_wT", "router_b", "w_in", "v_in", "w_out"]


def kernel(L0_attn_x, L0_attn_weight_qkv, L0_attn_out_w, L0_attn_out_b, L0_ffn_router_w, L0_ffn_router_b,
           L0_ffn_W, L0_ffn_V, L0_ffn_W_out):
    import numpy as _np
    import concourse.bacc as _bacc
    from concourse import mybir as _mybir
    from concourse.bass_utils import run_bass_kernel_spmd as _run

    given = [L0_attn_x, L0_attn_weight_qkv, _np.asarray(L0_attn_out_w).T, L0_attn_out_b,
             _np.asarray(L0_ffn_router_w).T, L0_ffn_router_b, L0_ffn_W, L0_ffn_V, L0_ffn_W_out]
    nc = _bacc.Bacc("TRN2", target_bir_lowering=False, num_devices=1)
    arrays, args = {}, []
    for name, a in zip(_INS, given):
        a = _np.ascontiguousarray(a)
        arrays[f"in_{name}"] = a
        args.append(nc.dram_tensor(f"in_{name}", a.shape, _mybir.dt.from_np(a.dtype), kind="ExternalInput").ap())
    args.append(nc.dram_tensor("out", arrays["in_x"].shape, F32, kind="ExternalOutput").ap())
    block_kernel(nc, *args)
    r = _run(nc, [arrays], core_ids=[0])
    return r.results[0]["out"]
```

```python
from contextlib import ExitStack

import concourse.bass as bass
from concourse import mybir

F32 = mybir.dt.float32
F16 = mybir.dt.float16
I32 = mybir.dt.int32
ALU = mybir.AluOpType
ACT = mybir.ActivationFunctionType
AX = mybir.AxisListType.X

P = 128
EPS = 1e-5
HI, LO = 0, 1
W_SCALE = 64.0
BIG = 3.0e38
STEPS = 4


def block_kernel(nc, x, w_qkv, out_wT, out_b, router_wT, router_b, w_in, v_in, w_out, out):
    B, T, D = x.shape
    N = B * T
    NT = N // P
    BT = T // P
    E, _, H = w_in.shape
    HB = H // P
    CAP = 2 * 512 * 2 // E
    CB = CAP // P
    NS = E * CB
    LOW = D // 4
    G = 4
    NG = NT // G
    ITS = NT // STEPS
    GC = G * P
    EB = P // NT
    NB = E // EB
    RC = 2 * P + 2
    assert NS // 2 == EB * CB and EB == STEPS and D == P and HB == 2 and CB == 2 and BT == 8 and B == 4

    Q_EVAC = 4.0 / (float(D) ** 0.5 * W_SCALE)
    K_SCALE = 1.0 / 4.0
    V_EVAC = 1.0 / W_SCALE

    xg_dram = nc.dram_tensor("xn_hi_lo", (N, 2 * D), F16, kind="Internal").ap()
    sum_dram = nc.dram_tensor("x_bias_experts", (N + CAP, D), F32, kind="Internal").ap()

    with ExitStack() as ctx:
        def sb(name, shape, dt=F32):
            return ctx.enter_context(nc.sbuf_tensor(name, shape, dt))

        def psum(name, shape):
            return ctx.enter_context(nc.psum_tensor(name, shape, F32))

        def sem(name):
            return ctx.enter_context(nc.semaphore(name))

        psS = psum("psS", [P, 2, 2, 512])
        psT = psum("psT", [P, 2, 512])
        psO = psum("psO", [P, 512])
        psM = psum("psM", [P, 512])

        x_sb = sb("x_sb", [P, NT, D])
        probs = sb("probs", [P, 2, T])
        xhl = sb("xhl", [P, NT, 2 * D], F16)
        QB = B - 2
        q_full = xhl[:, 0:QB * BT, :].rearrange("p n d -> p (n d)").bitcast(F32)
        xT = sb("xT", [P, 2, N], F16)
        qT = sb("qT", [P, 2, N], F16)
        kT = sb("kT", [P, 2, N], F16)
        vp = sb("vp", [P, NT, 2, D], F16)
        attn = sb("attn", [P, NT, D])
        attn_flat = attn[:].rearrange("p n d -> p (n d)")
        qkv_in = attn_flat[:, 0:3 * D]
        owT_in = attn_flat[:, 3 * D:4 * D]
        VB = B - 1
        v_full = attn_flat[:, N - VB * T:N].rearrange("p (n d) -> p n d", d=D)
        w_hl, wT = (attn_flat[:, c * D:(c + 3) * D].bitcast(F16).rearrange("p (s c) -> p s c", s=2) for c in (4, 7))
        shared = sb("shared", [P, 4096])
        wv_in = shared[:].rearrange("p (e h) -> p e h", e=E)
        half = NS * D
        xg = shared[:, 0:half].bitcast(F16).rearrange("p (s c) -> p s c", s=NS)
        y_sb = shared[:, half:2 * half].rearrange("p (s d) -> p s d", s=NS)
        wv = sb("wv", [P, 2, E, 2 * H], F16)
        wo_in = sb("wo_in", [P, E, HB * D])
        wo = sb("wo", [P, 2, E, HB * D], F16)
        pT = sb("pT", [P, 2, 2, T], F16)
        fused = sb("fused", [P, 2, 2 * D], F16)
        fused_mid = sb("fused_mid", [P, 2 * D], F16)
        mid = sb("mid", [P, 1])
        mid_k = sb("mid_k", [P, 1])
        owT = sb("owT", [P, 2, D], F16)
        rw_in = sb("rw_in", [P, E])
        rw = sb("rw", [P, 2, E], F16)
        rb = sb("rb", [P, E])
        bias = sb("bias", [P, D])

        ident = sb("ident", [P, P])
        ident16 = sb("ident16", [P, P], F16)
        upper = sb("upper", [P, P], F16)
        below = sb("below", [P, P], F16)
        slot_i = sb("slot_i", [P, CAP], I32)
        slot_row = sb("slot_row", [P, CAP], F16)
        slot_col_i = sb("slot_col_i", [P, NS], I32)
        slot_col = sb("slot_col", [P, NS])
        slot_next = sb("slot_next", [P, NS])
        slot_dump = sb("slot_dump", [P, NS])
        rank_i = sb("rank_i", [P, E], I32)
        rank = sb("rank", [P, E])
        tile_i = sb("tile_i", [P, 1], I32)

        stats = sb("stats", [P, NT, 6])
        mv = sb("mv", [P, NT, 2])
        std = sb("std", [P, NT])
        rstd = sb("rstd", [P, NT])

        logits, rest, first, second, ta = (sb(name, [P, NT, E]) for name in ("logits", "rest", "first", "second", "ta"))
        top1 = sb("top1", [P, NT])
        top2 = sb("top2", [P, NT])
        pick = sb("pick", [P, NT])
        gap = sb("gap", [P, NT])
        egap = sb("egap", [P, NT])
        gate1 = sb("gate1", [P, NT])
        gate2 = sb("gate2", [P, NT])
        mask = sb("mask", [P, E, NT], F16)
        gates = sb("gates", [P, E, NT])
        tot = sb("tot", [P, NB], F16)
        start = sb("start", [P, NB])
        end = sb("end", [P, NB])
        before_end = sb("before_end", [P, NB, CAP], F16)
        in_tile = sb("in_tile", [P, NB, CAP], F16)
        own = sb("own", [P, EB, NB, CAP], F16)
        row_src = sb("row_src", [P, NB, RC], F16)
        row_lo = sb("row_lo", [P, NB, P], F16)
        row = sb("row", [P, 4, RC])
        count = sb("count", [P, NS])
        aux = sb("aux", [P, NS, 2])
        slot_w = sb("slot_w", [P, NS])
        slot_ws = sb("slot_ws", [P, NS])
        unused = sb("unused", [P, NS])
        where = sb("where", [P, NS])
        to_row = sb("to_row", [P, NS], I32)
        from_row = sb("from_row", [P, NS], I32)

        neg_max = sb("neg_max", [P, 4])
        row_sum = sb("row_sum", [P, 4])
        inv_sum = sb("inv_sum", [P, 4])

        xT_flat = xT[:].rearrange("p s n -> p (s n)")
        assert 14 * HB * CAP <= 2 * N

        def after_xT(k, size, dt=F16):
            return xT_flat[:, k * HB * CAP:k * HB * CAP + size].bitcast(dt) if dt != F16 else \
                xT_flat[:, k * HB * CAP:k * HB * CAP + size]

        HC = HB * CAP
        xgT = after_xT(0, 4 * CAP).rearrange("p (q s c) -> p q s c", q=2, s=2)
        hidT = after_xT(2, 4 * HC).rearrange("p (q s c) -> p q s c", q=2, s=2)
        hid = after_xT(6, 4 * HC, F32).rearrange("p (q c) -> p q c", q=2)
        silu = after_xT(10, 2 * HC, F32)
        tanh_b = after_xT(12, 2 * HC, F32)

        x_in = [sem(f"x_in{b}") for b in range(B)]
        x_half = sem("x_half")
        small_in, rows_in, w_in_s, wo_in_s = sem("small_in"), sem("rows_in"), sem("w_in"), sem("wo_in")
        zeroed, consts_i, consts = sem("zeroed"), sem("consts_i"), sem("consts")
        stat_s, var_s, std_s, rstd_s, xn_s = sem("stat"), sem("var"), sem("std"), sem("rstd"), sem("xn")
        x_hi, x_lo = sem("x_hi"), sem("x_lo")
        xb_s, xb_out, xg_out = sem("xb"), sem("xb_out"), [sem(f"xg_out{i}") for i in range(2)]
        mid_s, small_hi, small_lo, band_lo = sem("mid"), sem("small_hi"), sem("small_lo"), sem("band_lo")
        wT_ps, wT_s, fused_ps, fused_s = sem("wT_ps"), sem("wT"), sem("fused_ps"), sem("fused")
        k_s = sem("k")
        wv_hi, wv_lo, wo_hi, wo_lo, w_up = sem("wv_hi"), sem("wv_lo"), sem("wo_hi"), sem("wo_lo"), sem("w_up")
        xT_ps, xT_s = sem("xT_ps"), sem("xT")
        scores_r = sem("router_scores")
        route = sem("route")
        gate_s, gates_s = sem("gate"), sem("gates")
        gap_s, egap_s, plan_in = sem("gap"), sem("egap"), sem("plan_in")
        counts_ps, all_counts_ps, end_s, gates_ps = sem("counts_ps"), sem("all_counts_ps"), sem("end"), sem("gates_ps")
        row_hi, row_counts, tot_s, in_tile_s, own_s, plan_s = (sem("row_hi"), sem("row_counts"), sem("tot"), sem("in_tile"), sem("own"),
                                                        sem("plan"))
        unit_ps, unit_hi, query_lo, value_lo, split_v, split_q = sem("unit_ps"), sem("unit_hi"), sem("query_lo"), sem("value_lo"), sem("split_v"), sem("split_q")
        s_ready, max_done, exp_done = sem("s_ready"), sem("max_done"), sem("exp_done")
        pt_ready, hi_done, lo_done = sem("pt_ready"), sem("hi_done"), sem("lo_done")
        pv_done, inv_done, o_done = sem("pv_done"), sem("inv_done"), sem("o_done")
        row_ps, row_sb, row_used, list_step, weights_s = (sem("row_ps"), sem("row_sb"), sem("row_used"), sem("list_step"),
                                                      sem("slot_weights"))
        gathered = [sem(f"gathered{i}") for i in range(E // 2)]
        pair_in = sem("pair_in")
        tt_ps, xgT_s = sem("tt_ps"), sem("xgT")
        b_ps, tanh_s, silu_s = sem("b_ps"), sem("tanh_b"), sem("silu")
        a_ps, hid_s, hid_hi, hid_lo = sem("a_ps"), sem("hid"), sem("hid_hi"), sem("hid_lo")
        y_ps, y_s, added = sem("y_ps"), sem("y"), sem("added")
        sum_in = [sem(f"sum_in{i}") for i in range(2)]
        final, out_s = sem("final"), sem("out")

        XT_CREDIT, PV_CREDIT, O_CREDIT, ROW_CREDIT, USED_CREDIT, Y_CREDIT = 2, 1, 1, 1, 4, 1

        x_t = x.rearrange("b (n p) d -> p (b n) d", p=P)
        out_t = out.rearrange("b (n p) d -> p (b n) d", p=P)
        sum_t = sum_dram.rearrange("(n p) d -> p n d", p=P)
        xg_t = xg_dram.rearrange("(n p) c -> p n c", p=P)

        block = ctx.enter_context(nc.Block())

        @block.sync
        def _(sp):
            sp.dma_start(x_sb[:, 0:G, :], x_t[:, 0:G, :]).then_inc(x_in[0], 16)
            sp.dma_start(x_sb[:, G:BT, :], x_t[:, G:BT, :]).then_inc(x_half, 16)
            for b in range(1, B):
                sp.dma_start(x_sb[:, b * BT:(b + 1) * BT, :], x_t[:, b * BT:(b + 1) * BT, :]).then_inc(x_in[b], 16)
            sp.dma_start(rb[:], router_b.rearrange("(a e) -> a e", a=1).to_broadcast([P, E])).then_inc(rows_in, 16)
            sp.dma_start(bias[:], out_b.rearrange("(a d) -> a d", a=1).to_broadcast([P, D])).then_inc(rows_in, 16)
            sp.dma_start(wo_in[:].rearrange("p e (c d) -> p e c d", c=HB),
                         w_out.rearrange("e (c p) d -> p e c d", p=P)).then_inc(wo_in_s, 16)
            sp.dma_start(wv_in[:, :, 0:H], w_in.rearrange("e d h -> d e h")).then_inc(w_in_s, 16)
            sp.dma_start(wv_in[:, :, H:2 * H], v_in.rearrange("e d h -> d e h")).then_inc(w_in_s, 16)
            for b in range(B):
                sp.wait_ge(x_lo, 2 * (b + 1))
                sp.dma_start(xg_t[:, b * BT:(b + 1) * BT, :], xhl[:, b * BT:(b + 1) * BT, :]).then_inc(xg_out[b // QB], 16)
            for b in range(B):
                sp.wait_ge(xb_s, b + 1)
                sp.dma_start(sum_t[:, b * BT:(b + 1) * BT, :], x_sb[:, b * BT:(b + 1) * BT, :]).then_inc(xb_out, 16)
            sp.dma_start(sum_t[:, NT:NT + CB, :], x_sb[:, 0:CB, :]).then_inc(xb_out, 16)
            sp.wait_ge(added, 16 * NS)
            m = (ITS - 1) * STEPS
            sp.dma_start(x_sb[:, 0:m, :], sum_t[:, 0:m, :]).then_inc(sum_in[0], 16)
            sp.dma_start(x_sb[:, m:NT, :], sum_t[:, m:NT, :]).then_inc(sum_in[1], 16)
            for it in range(ITS - 1):
                t = it * STEPS
                sp.wait_ge(final, it + 1)
                sp.dma_start(out_t[:, t:t + STEPS, :], attn[:, t:t + STEPS, :]).then_inc(out_s, 16)
            for s in range(STEPS):
                t = m + s
                sp.wait_ge(o_done, t + 1 + O_CREDIT)
                sp.dma_start(out_t[:, t, :], attn[:, t, :]).then_inc(out_s, 16)
            sp.wait_ge(out_s, 16 * (ITS - 1 + STEPS))
            for done in xg_out:
                sp.wait_ge(done, 16 * QB)

        @block.scalar
        def _(act):
            act.dma_start(qkv_in, w_qkv).then_inc(small_in, 16)
            act.dma_start(owT_in, out_wT).then_inc(small_in, 16)
            act.dma_start(rw_in[:], router_wT).then_inc(small_in, 16)
            act.preload_act_table(ACT.Sqrt)

            def std_of(b):
                act.wait_ge(var_s, b + 1)
                act.activation(std[:, b * BT:(b + 1) * BT], mv[:, b * BT:(b + 1) * BT, 1], ACT.Sqrt).then_inc(std_s, 1)

            def x_high(b):
                for h in range(2):
                    t = b * BT + h * G
                    act.wait_ge(xn_s, b + 1)
                    act.activation(xhl[:, t:t + G, 0:D], probs[:, b % 2, h * GC:(h + 1) * GC].rearrange(
                        "p (n d) -> p n d", n=G), ACT.Copy).then_inc(x_hi, 1)

            def turned(b):
                for h in range(2):
                    g = 2 * b + h
                    act.wait_ge(xT_ps, g + 1)
                    act.activation(xT[:, :, g * GC:(g + 1) * GC], psT[:, h, :].bitcast(F16).rearrange(
                        "p (s c) -> p s c", s=2), ACT.Copy).then_inc(xT_s, 1)

            def unit_high(b):
                for h in range(2):
                    g = 2 * b + h
                    act.wait_ge(unit_ps, 2 * g + 1)
                    f = g * GC - (B - QB) * T
                    dst = qT[:, HI, g * GC:(g + 1) * GC] if b < B - QB else q_full[:, f:f + GC]
                    act.activation(dst, psS[:, h, 0, :], ACT.Copy, scale=Q_EVAC).then_inc(unit_hi, 1)
                    act.wait_ge(unit_ps, 2 * g + 2)
                    f = g * G - (NT - VB * BT)
                    dst = vp[:, g * G:(g + 1) * G, HI, :] if b < B - VB else v_full[:, f:f + G, :]
                    act.activation(dst, psS[:, h, 1, :].rearrange("p (n d) -> p n d", n=G), ACT.Copy,
                                   scale=V_EVAC).then_inc(unit_hi, 1)

            std_of(0)
            act.wait_ge(small_in, 48)
            act.activation(w_hl[:, HI, :], qkv_in, ACT.Copy, scale=W_SCALE).then_inc(small_hi, 1)
            act.activation(owT[:, HI, :], owT_in, ACT.Copy, scale=W_SCALE).then_inc(small_hi, 1)
            act.activation(rw[:, HI, :], rw_in[:], ACT.Copy, scale=W_SCALE).then_inc(small_hi, 1)
            x_high(0)
            act.wait_ge(wT_ps, 1)
            act.activation(wT, psS[:, 0, 0, 0:3 * D].bitcast(F16).rearrange("p (s c) -> p s c", s=2), ACT.Copy).then_inc(wT_s, 1)
            std_of(1)
            turned(0)
            act.wait_ge(fused_ps, 1)
            act.activation(fused[:, HI, :], psO[:, 0:2 * D], ACT.Copy, scale=1.0 / W_SCALE).then_inc(fused_s, 1)
            x_high(1)
            std_of(2)
            turned(1)
            x_high(2)
            std_of(3)
            unit_high(0)
            x_high(3)
            turned(2)
            unit_high(1)
            turned(3)
            act.wait_ge(xg_out[0], 16 * QB)
            unit_high(2)
            unit_high(3)
            act.preload_act_table(ACT.Exp)

            def expert_weights_high(c):
                ce = slice(2 * c, 2 * c + 2)
                act.activation(wv[:, HI, ce, :], wv_in[:, ce, :], ACT.Copy, scale=W_SCALE).then_inc(wv_hi, 1)

            act.wait_ge(w_in_s, 32)

            def exp_of(i, par):
                act.wait_ge(max_done, i + 1)
                act.activation(probs[:, par % 2, :], psS[:, par % 2].rearrange("p a c -> p (a c)"), ACT.Exp,
                               bias=neg_max[:, par % 4:par % 4 + 1],
                               accum_out=row_sum[:, par % 4:par % 4 + 1]).then_inc(exp_done, 1)

            def probs_high(i, par):
                for h in range(2):
                    act.wait_ge(pt_ready, 2 * i + h + 1)
                    if h == 0:
                        act.wait_ge(pv_done, i - 1 + PV_CREDIT)
                    act.activation(pT[:, par % 2, HI, h * 512:(h + 1) * 512], psT[:, h, :], ACT.Copy).then_inc(hi_done, 1)

            def scale_out(i, par):
                act.wait_ge(inv_done, i + 1)
                act.wait_ge(pv_done, i + 1 + PV_CREDIT)
                act.activation(attn[:, bass.ds(i, 1), :].rearrange("p a d -> p (a d)"), psO[:, 0:D], ACT.Copy,
                               scale=inv_sum[:, par % 4:par % 4 + 1]).then_inc(o_done, 1)

            def row_out(e, s, j):
                u = 2 * e + j
                act.wait_ge(row_ps, u + 1)
                act.wait_ge(row_used, u + 1 - 4 + USED_CREDIT)
                act.activation(row[:, (2 * s + j) % 4, :], psM[:, 0:RC], ACT.Copy).then_inc(row_sb, 1)

            def tanh_of(e):
                act.wait_ge(b_ps, e + 1)
                act.activation(tanh_b, psM[:], ACT.Tanh, scale=0.5 / W_SCALE).then_inc(tanh_s, 1)

            def hid_high(e, q):
                act.wait_ge(hid_s, e + 1)
                act.activation(hidT[:, q, HI, :], hid[:, q, :], ACT.Copy).then_inc(hid_hi, 1)

            def y_out(e):
                act.wait_ge(y_ps, e + 1)
                for j in range(CB):
                    ins = act.activation(y_sb[:, bass.ds(2 * e + j, 1), :].rearrange("p a d -> p (a d)"),
                                         psM[:, j * D:(j + 1) * D], ACT.Copy,
                                         scale=slot_ws[:, bass.ds(2 * e + j, 1)])
                ins.then_inc(y_s, 1)

            def steps(it, lists=False, experts=False, last=False):
                for s in range(STEPS):
                    i = it * STEPS + s
                    e0 = 2 * (it - 2)
                    if lists:
                        row_out(4 * it + s, s, 0)
                    if experts and s in (2, 3):
                        hid_high(e0 + s - 2, s - 2)
                    if experts and s in (1, 2):
                        tanh_of(e0 + s - 1)
                    if not last or s < STEPS - 1:
                        probs_high(i + 1, s + 1)
                    if experts and s == 3:
                        y_out(e0)
                    if lists:
                        row_out(4 * it + s, s, 1)
                    if not last or s < STEPS - 2:
                        exp_of(i + 2, s + 2)
                    if lists:
                        scale_out(i, s)
                    if experts and s == 3:
                        y_out(e0 + 1)

            expert_weights_high(0)
            expert_weights_high(1)
            act.wait_ge(gap_s, 2)
            act.activation(egap[:], gap[:], ACT.Exp).then_inc(egap_s, 1)
            exp_of(0, 0)
            expert_weights_high(2)
            exp_of(1, 1)
            for h in range(2):
                act.wait_ge(pt_ready, h + 1)
                act.activation(pT[:, 0, HI, h * 512:(h + 1) * 512], psT[:, h, :], ACT.Copy).then_inc(hi_done, 1)
            act.wait_ge(end_s, 1)
            act.activation(row_src[:, :, 0:P], psM[:, 0:NB * P].rearrange("p (h t) -> p h t", h=NB),
                           ACT.Copy).then_inc(row_counts, 1)
            act.wait_ge(gates_ps, 1)
            act.activation(row_src[:, :, P:2 * P], psO[:, 0:NB * P].rearrange("p (h t) -> p h t", h=NB),
                           ACT.Copy).then_inc(row_hi, 1)
            act.wait_ge(in_tile_s, NB)
            act.wait_ge(zeroed, 5)
            for e in range(EB):
                rows = slice(e * NT, (e + 1) * NT)
                ins = act.activation(own[rows, e, :, :], in_tile[rows], ACT.Copy)
            ins.then_inc(own_s, 1)
            expert_weights_high(3)
            with act.Fori(0, 2) as it:
                steps(it, lists=True)
            act.wait_ge(weights_s, 2)
            with act.Fori(1, 3) as pair:
                steps(2 * pair, experts=True)
                steps(2 * pair + 1, experts=True)
            steps(6)
            steps(7, last=True)

        @block.vector
        def _(dve):
            dve.memset(mid[:], 0.0).then_inc(mid_s, 1)
            dve.memset(mid_k[:], 0.0).then_inc(mid_s, 1)
            dve.memset(neg_max[:], 0.0).then_inc(xT_s, XT_CREDIT)
            dve.memset(row_sum[:], 0.0)
            dve.memset(inv_sum[:], 0.0).then_inc(pv_done, PV_CREDIT)
            dve.memset(count[:], 0.0).then_inc(o_done, O_CREDIT)
            dve.memset(aux[:], 0.0).then_inc(row_sb, ROW_CREDIT)
            dve.memset(slot_w[:], 0.0).then_inc(row_used, USED_CREDIT)
            dve.memset(unused[:], 0.0).then_inc(y_s, Y_CREDIT)
            dve.wait_ge(mid_s, 2)
            for m0 in (LOW, 2 * LOW):
                dve.memset(mid[m0:m0 + LOW], 1.0).then_inc(mid_s, 1)
                dve.memset(mid_k[m0:m0 + LOW], K_SCALE).then_inc(mid_s, 1)

            def stats_of(b):
                dve.wait_ge(x_in[b], 16)
                for t in range(b * BT, (b + 1) * BT):
                    if t == G:
                        dve.wait_ge(x_half, 16)
                    ins = dve.bn_stats(stats[:, t, :], x_sb[:, t, :])
                ins.then_inc(stat_s, 1)
                dve.wait_ge(stat_s, 2 * b + 1)
                for t in range(b * BT, (b + 1) * BT):
                    ins = dve.bn_aggr(mv[:, t, :], stats[:, t, :])
                ins.then_inc(stat_s, 1)
                dve.wait_ge(stat_s, 2 * b + 2)
                v = mv[:, b * BT:(b + 1) * BT, 1]
                dve.tensor_scalar(v, v, EPS, None, ALU.add).then_inc(var_s, 1)

            def normalise(b):
                dve.wait_ge(std_s, b + 1)
                dve.reciprocal(rstd[:, b * BT:(b + 1) * BT], std[:, b * BT:(b + 1) * BT]).then_inc(rstd_s, 1)
                dve.wait_ge(rstd_s, b + 1)
                if b >= 2:
                    dve.wait_ge(x_lo, 2 * (b - 1))
                for k in range(BT):
                    t = b * BT + k
                    ins = dve.tensor_scalar(probs[:, b % 2, k * D:(k + 1) * D], x_sb[:, t, :], mv[:, t, 0:1],
                                            rstd[:, t:t + 1], ALU.subtract, ALU.mult)
                ins.then_inc(xn_s, 1)

            def unit_low(b, halves=(0, 1)):
                for h in halves:
                    g = 2 * b + h
                    at = slice(g * GC, (g + 1) * GC)
                    if b < B - QB:
                        dve.wait_ge(unit_hi, 2 * g + 1)
                        dve.scalar_tensor_tensor(out=qT[:, LO, at], in0=psS[:, h, 0, :], scalar=Q_EVAC, in1=qT[:, HI, at],
                                                 op0=ALU.mult, op1=ALU.subtract).then_inc(query_lo, 1)
                    if b < B - VB:
                        at = slice(g * G, (g + 1) * G)
                        dve.wait_ge(unit_hi, 2 * g + 2)
                        dve.scalar_tensor_tensor(out=vp[:, at, LO, :], in0=psS[:, h, 1, :].rearrange(
                            "p (n d) -> p n d", n=G), scalar=V_EVAC, in1=vp[:, at, HI, :], op0=ALU.mult,
                            op1=ALU.subtract).then_inc(value_lo, 1)

            dve.wait_ge(consts_i, 4)
            dve.tensor_copy(slot_row[:], slot_i[:])
            dve.tensor_copy(slot_col[:], slot_col_i[:])
            dve.tensor_scalar(slot_next[:], slot_col_i[:], 1.0, None, ALU.add)
            dve.tensor_scalar(slot_dump[:], slot_col_i[:], float(N - P), None, ALU.add)
            dve.tensor_copy(rank[:], rank_i[:])
            for h in range(NB):
                dve.memset(row_src[:, h, 2 * P + 1:RC], 1.0)
                for e in range(EB):
                    rows = slice(e * NT, (e + 1) * NT)
                    ins = dve.tensor_scalar(row_src[rows, h, 2 * P:2 * P + 1], tile_i[rows], float(-e * N), None, ALU.add)
            ins.then_inc(consts, 1)
            stats_of(0)
            normalise(0)
            dve.wait_ge(small_hi, 3)
            for w_in_f32, hi, lo in ((qkv_in, w_hl[:, HI, :], w_hl[:, LO, :]), (owT_in, owT[:, HI, :], owT[:, LO, :]),
                                     (rw_in[:], rw[:, HI, :], rw[:, LO, :])):
                dve.scalar_tensor_tensor(out=lo, in0=w_in_f32, scalar=W_SCALE, in1=hi, op0=ALU.mult,
                                         op1=ALU.subtract).then_inc(small_lo, 1)
            dve.wait_ge(mid_s, 6)
            dve.wait_ge(small_lo, 3)
            dve.tensor_scalar(w_hl[:, LO, :], w_hl[:, LO, :], mid[:, 0:1], None, ALU.mult).then_inc(band_lo, 1)
            stats_of(1)
            normalise(1)
            dve.wait_ge(fused_s, 1)
            dve.scalar_tensor_tensor(out=fused[:, LO, :], in0=psO[:, 0:2 * D], scalar=1.0 / W_SCALE, in1=fused[:, HI, :],
                                     op0=ALU.mult, op1=ALU.subtract).then_inc(fused_s, 1)
            dve.tensor_scalar(fused_mid[:], fused[:, HI, :], mid[:, 0:1], None, ALU.mult).then_inc(fused_s, 1)
            stats_of(2)
            normalise(2)
            stats_of(3)
            normalise(3)
            unit_low(0)

            def max_of(i, par):
                dve.wait_ge(s_ready, i + 1)
                dve.tensor_reduce(neg_max[:, par % 4:par % 4 + 1], psS[:, par % 2].rearrange("p a c -> p (a c)"),
                                  AX, ALU.max, negate=True).then_inc(max_done, 1)

            def probs_low(i, par):
                for h in range(2):
                    cols = slice(h * 512, (h + 1) * 512)
                    dve.wait_ge(hi_done, 2 * i + h + 1)
                    dve.tensor_tensor(pT[:, par % 2, LO, cols], psT[:, h, :], pT[:, par % 2, HI, cols],
                                      ALU.subtract).then_inc(lo_done, 1)

            n = [0]

            def then(ins):
                n[0] += 1
                ins.then_inc(route, 1)
                dve.wait_ge(route, n[0])

            def over_e(a, t=slice(0, NT)):
                return a[:, t].unsqueeze(2).to_broadcast([P, t.stop - t.start, E])

            EARLY, LATE = slice(0, NT // 2), slice(NT // 2, NT)

            def per_tile(a, t):
                return a[:].unsqueeze(1).to_broadcast([P, t.stop - t.start, E])

            def top_scores(t, bank):
                dve.wait_ge(scores_r, t.stop // G)
                count = (t.stop - t.start) * E
                then(dve.scalar_tensor_tensor(out=logits[:, t], in0=bank[:, 0:count].rearrange("p (n e) -> p n e", e=E),
                                              scalar=1.0 / W_SCALE, in1=per_tile(rb, t), op0=ALU.mult, op1=ALU.add))
                then(dve.tensor_reduce(top1[:, t], logits[:, t], AX, ALU.max))
                then(dve.tensor_tensor(ta[:, t], logits[:, t], over_e(top1, t), ALU.is_equal))

            def first_expert(t, chosen):
                then(dve.tensor_tensor(ta[:, t], ta[:, t], per_tile(rank, t), ALU.mult))
                then(dve.tensor_reduce(pick[:, t], ta[:, t], AX, ALU.max))
                then(dve.tensor_tensor(chosen[:, t], per_tile(rank, t), over_e(pick, t), ALU.is_equal))

            def second_scores(t):
                then(dve.scalar_tensor_tensor(out=rest[:, t], in0=first[:, t], scalar=-BIG, in1=logits[:, t],
                                              op0=ALU.mult, op1=ALU.add))
                then(dve.tensor_reduce(top2[:, t], rest[:, t], AX, ALU.max))
                dve.tensor_tensor(gap[:, t], top2[:, t], top1[:, t], ALU.subtract).then_inc(gap_s, 1)
                then(dve.tensor_tensor(ta[:, t], rest[:, t], over_e(top2, t), ALU.is_equal))

            def mark_tokens(t):
                dve.tensor_tensor(mask[:, :, t].rearrange("p e n -> p n e"), first[:, t], second[:, t],
                                  ALU.add).then_inc(plan_in, 1)

            dve.wait_ge(rows_in, 32)
            dve.wait_ge(consts, 1)
            top_scores(EARLY, psM)
            unit_low(1, (0,))
            first_expert(EARLY, first)
            unit_low(1, (1,))
            second_scores(EARLY)
            first_expert(EARLY, second)
            mark_tokens(EARLY)
            top_scores(LATE, psO)
            first_expert(LATE, first)
            second_scores(LATE)
            first_expert(LATE, second)
            mark_tokens(LATE)
            max_of(0, 0)
            dve.wait_ge(counts_ps, 1)
            counts = psM[:, 0:NB * P].rearrange("p (h t) -> p h t", h=NB)
            dve.tensor_copy(tot[:], counts[:, :, P - 1]).then_inc(tot_s, 1)
            dve.wait_ge(egap_s, 1)
            then(dve.tensor_scalar(pick[:], egap[:], 1.0, None, ALU.add))
            dve.reciprocal(gate1[:], pick[:]).then_inc(gate_s, 1)
            max_of(1, 1)
            dve.wait_ge(all_counts_ps, 1)
            dve.tensor_copy(end[:], counts[:, :, P - 1]).then_inc(end_s, 1)
            dve.wait_ge(end_s, 1)
            dve.tensor_tensor(start[:], end[:], tot[:], ALU.subtract)
            for h in range(NB):
                ins = dve.tensor_scalar(before_end[:, h, :], slot_row[:], end[:, h:h + 1], None, ALU.is_lt)
            then(ins)
            for h in range(NB):
                ins = dve.scalar_tensor_tensor(out=in_tile[:, h, :], in0=slot_row[:], scalar=start[:, h:h + 1],
                                               in1=before_end[:, h, :], op0=ALU.is_ge, op1=ALU.mult).then_inc(in_tile_s, 1)
            probs_low(0, 0)
            dve.wait_ge(row_hi, 1)
            dve.tensor_tensor(row_lo[:], psO[:, 0:NB * P].rearrange("p (h t) -> p h t", h=NB),
                              row_src[:, :, P:2 * P], ALU.subtract).then_inc(plan_s, 1)

            def invert_sum(i, par):
                c = slice(par % 4, par % 4 + 1)
                dve.wait_ge(exp_done, i + 1)
                dve.reciprocal(inv_sum[:, c], row_sum[:, c]).then_inc(inv_done, 1)

            def scale_out(i, par, last):
                c = slice(par % 4, par % 4 + 1)
                dve.wait_ge(inv_done, i + 1)
                dve.wait_ge(pv_done, i + 1 + PV_CREDIT)
                if last:
                    dve.wait_ge(sum_in[1], 16)
                    dve.scalar_tensor_tensor(out=attn[:, i, :], in0=psO[:, 0:D], scalar=inv_sum[:, c],
                                             in1=x_sb[:, i, :], op0=ALU.mult, op1=ALU.add).then_inc(o_done, 1)
                else:
                    dve.tensor_scalar(attn[:, bass.ds(i, 1), :].rearrange("p a d -> p (a d)"), psO[:, 0:D],
                                      inv_sum[:, c], None, ALU.mult).then_inc(o_done, 1)

            def row_read(e, s, j):
                u = 2 * e + j
                r = row[:, (2 * s + j) % 4, :]
                dve.wait_ge(row_sb, u + 1 + ROW_CREDIT)
                dve.scalar_tensor_tensor(out=r[:, P:2 * P], in0=r[:, 0:P], scalar=slot_next[:, j:j + 1],
                                         in1=r[:, P:2 * P], op0=ALU.is_equal, op1=ALU.mult,
                                         accum_out=slot_w[:, bass.ds(u, 1)])
                dve.tensor_scalar(r[:, 0:P], r[:, 0:P], slot_col[:, j:j + 1], None, ALU.is_le, ALU.add,
                                  accum_out=count[:, bass.ds(u, 1)])
                dve.tensor_copy(aux[:, bass.ds(u, 1), :].rearrange("p a c -> p (a c)"), r[:, 2 * P:RC]).then_inc(row_used, 1)

            def gate_of(e):
                dve.wait_ge(tanh_s, e + 1)
                dve.scalar_tensor_tensor(out=silu, in0=tanh_b, scalar=1.0, in1=psM[:], op0=ALU.add,
                                         op1=ALU.mult).then_inc(silu_s, 1)

            def hidden_of(e, q):
                dve.wait_ge(a_ps, e + 1)
                dve.wait_ge(silu_s, e + 1)
                dve.scalar_tensor_tensor(out=hid[:, q, :], in0=psM[:], scalar=0.5 / (W_SCALE * W_SCALE), in1=silu,
                                         op0=ALU.mult, op1=ALU.mult).then_inc(hid_s, 1)

            def steps(it, lists=False, experts=False, last=False):
                for s in range(STEPS):
                    i = it * STEPS + s
                    e0 = 2 * (it - 2)
                    if experts and s in (2, 3):
                        hidden_of(e0 + s - 2, s - 2)
                    if not last or s < STEPS - 2:
                        max_of(i + 2, s + 2)
                    if experts and s in (1, 2):
                        gate_of(e0 + s - 1)
                    if not last or s < STEPS - 1:
                        probs_low(i + 1, s + 1)
                    if lists:
                        row_read(4 * it + s, s, 0)
                    if lists:
                        row_read(4 * it + s, s, 1)
                    invert_sum(i, s)
                    if not lists:
                        scale_out(i, s, last)
                    if experts and s == 0:
                        dve.wait_ge(tt_ps, it - 2 + 1)
                        dve.tensor_copy(xgT, psM[:].bitcast(F16).rearrange("p (q s c) -> p q s c", q=2, s=2)).then_inc(xgT_s, 1)

            with dve.Fori(0, 2) as it:
                steps(it, lists=True)
            with dve.Fori(1, 3) as pair:
                steps(2 * pair, experts=True)
                steps(2 * pair + 1, experts=True)
            steps(6)
            steps(7, last=True)

        @block.gpsimd
        def _(pool):
            pool.iota(slot_i[:], [[1, CAP]], base=0, channel_multiplier=0).then_inc(consts_i, 1)
            pool.iota(slot_col_i[:].rearrange("p (e j) -> p e j", j=CB), [[0, E], [P, CB]], base=0,
                      channel_multiplier=1).then_inc(consts_i, 1)
            pool.iota(rank_i[:], [[-1, E]], base=E, channel_multiplier=0).then_inc(consts_i, 1)
            pool.iota(tile_i[:], [[0, 1]], base=0, channel_multiplier=P).then_inc(consts_i, 1)
            pool.memset(ident16[:], 0.0).then_inc(zeroed, 1)
            pool.memset(ident[:], 0.0).then_inc(zeroed, 1)
            pool.memset(upper[:], 1.0).then_inc(zeroed, 1)
            pool.memset(below[:], 1.0).then_inc(zeroed, 1)
            pool.wait_ge(zeroed, 4)
            for t in (ident16, ident):
                pool.affine_select(out=t[:], in_=t[:], compare_op=ALU.not_equal, fill=1.0, base=0, pattern=[[-1, P]],
                                   channel_multiplier=1).then_inc(consts_i, 1)
            pool.affine_select(out=upper[:], in_=upper[:], compare_op=ALU.is_ge, fill=0.0, base=0, pattern=[[1, P]],
                               channel_multiplier=-1).then_inc(consts_i, 1)
            pool.affine_select(out=below[:], in_=below[:], compare_op=ALU.is_gt, fill=0.0, base=0, pattern=[[1, P]],
                               channel_multiplier=-1).then_inc(consts_i, 1)
            pool.wait_ge(consts_i, 8)
            for e in range(1, EB):
                pool.memset(below[0:e * NT, e * NT:(e + 1) * NT], 0.0).then_inc(consts_i, 1)
            pool.memset(own[:], 0.0).then_inc(zeroed, 1)
            def keys(b):
                at = slice(b * T, (b + 1) * T)
                pool.wait_ge(xT_s, 2 * (b + 1) + XT_CREDIT)
                pool.tensor_scalar(kT[:, HI, at], xT[:, HI, at], K_SCALE, 0.0, ALU.mult, ALU.add).then_inc(k_s, 1)
                pool.tensor_scalar(kT[:, LO, at], xT[:, LO, at], mid_k[:, 0:1], 0.0, ALU.mult, ALU.add).then_inc(k_s, 1)

            pool.wait_ge(mid_s, 6)
            for b in range(B):
                for h in range(2):
                    t = b * BT + h * G
                    pool.wait_ge(x_hi, 2 * b + h + 1)
                    pool.tensor_tensor(xhl[:, t:t + G, D:2 * D], probs[:, b % 2, h * GC:(h + 1) * GC].rearrange(
                        "p (n d) -> p n d", n=G), xhl[:, t:t + G, 0:D], ALU.subtract).then_inc(x_lo, 1)
            for b in range(B):
                keys(b)
            def gates_of_tokens():
                def over_e(a):
                    return a[:].unsqueeze(2).to_broadcast([P, NT, E])

                pool.wait_ge(gate_s, 1)
                pool.tensor_tensor(gate2[:], gate1[:], egap[:], ALU.mult).then_inc(gate_s, 1)
                pool.tensor_tensor(first[:], first[:], over_e(gate1), ALU.mult).then_inc(gate_s, 1)
                pool.wait_ge(gate_s, 2)
                pool.tensor_tensor(second[:], second[:], over_e(gate2), ALU.mult).then_inc(gate_s, 1)
                pool.wait_ge(gate_s, 4)
                pool.tensor_tensor(gates[:].rearrange("p e n -> p n e"), first[:], second[:], ALU.add).then_inc(gates_s, 1)

            pool.wait_ge(rows_in, 32)
            bias_b = bias[:].unsqueeze(1).to_broadcast([P, BT, D])
            for b in range(B):
                if b == 2:
                    gates_of_tokens()
                xb = x_sb[:, b * BT:(b + 1) * BT, :]
                pool.tensor_tensor(xb, xb, bias_b, ALU.add).then_inc(xb_s, 1)
            def split_w_out(c):
                ee = slice(c * (E // 2), (c + 1) * (E // 2))
                pool.tensor_scalar(wo[:, HI, ee], wo_in[:, ee], W_SCALE, 0.0, ALU.mult, ALU.add).then_inc(wo_hi, 1)
                pool.wait_ge(wo_hi, 2 * c + 1)
                pool.tensor_scalar(wo_in[:, ee], wo_in[:, ee], W_SCALE, 0.0, ALU.mult, ALU.add).then_inc(wo_hi, 1)
                pool.wait_ge(wo_hi, 2 * c + 2)
                pool.tensor_tensor(wo[:, LO, ee], wo_in[:, ee], wo[:, HI, ee], ALU.subtract).then_inc(wo_lo, 1)

            pool.wait_ge(wo_in_s, 16)
            split_w_out(0)

            def split_values(c):
                g = 2 * (B - VB) + c
                at, f = slice(g * G, (g + 1) * G), slice(c * G, (c + 1) * G)
                pool.wait_ge(unit_hi, 2 * g + 2)
                pool.tensor_scalar(vp[:, at, HI, :], v_full[:, f, :], 1.0, 0.0, ALU.mult, ALU.add).then_inc(split_v, 1)
                pool.wait_ge(split_v, 2 * c + 1)
                pool.tensor_tensor(vp[:, at, LO, :], v_full[:, f, :], vp[:, at, HI, :], ALU.subtract).then_inc(split_v, 1)

            pool.wait_ge(w_in_s, 32)
            for c in range(4):
                ce = slice(2 * c, 2 * c + 2)
                pool.wait_ge(wv_hi, c + 1)
                pool.tensor_scalar(wv_in[:, ce, :], wv_in[:, ce, :], W_SCALE, 0.0, ALU.mult, ALU.add).then_inc(w_up, 1)
                pool.wait_ge(w_up, c + 1)
                pool.tensor_tensor(wv[:, LO, ce, :], wv_in[:, ce, :], wv[:, HI, ce, :], ALU.subtract).then_inc(wv_lo, 1)

            def split_queries(b):
                for h in range(2):
                    c = 2 * (b - (B - QB)) + h
                    at, f = slice((2 * b + h) * GC, (2 * b + h + 1) * GC), slice(c * GC, (c + 1) * GC)
                    pool.wait_ge(unit_hi, 2 * (2 * b + h) + 1)
                    pool.tensor_scalar(qT[:, HI, at], q_full[:, f], 1.0, 0.0, ALU.mult, ALU.add).then_inc(split_q, 1)
                    pool.wait_ge(split_q, 2 * c + 1)
                    pool.tensor_tensor(qT[:, LO, at], q_full[:, f], qT[:, HI, at], ALU.subtract).then_inc(split_q, 1)

            def slot_lists(c):
                k = slice(c * (NS // 2), (c + 1) * (NS // 2))
                n = 6 * c
                pool.wait_ge(row_used, (c + 1) * (NS // 2) + USED_CREDIT)
                pool.tensor_scalar(slot_ws[:, k], slot_w[:, k], 1.0 / W_SCALE, None, ALU.mult).then_inc(weights_s, 1)
                pool.tensor_scalar(unused[:, k], aux[:, k, 1], -1.0, 1.0, ALU.mult, ALU.add).then_inc(list_step, 1)
                pool.tensor_tensor(where[:, k], aux[:, k, 0], count[:, k], ALU.add).then_inc(list_step, 1)
                pool.wait_ge(list_step, n + 2)
                pool.tensor_tensor(unused[:, k], unused[:, k], slot_dump[:, k], ALU.mult).then_inc(list_step, 1)
                pool.wait_ge(list_step, n + 3)
                pool.tensor_tensor(where[:, k], where[:, k], unused[:, k], ALU.add).then_inc(list_step, 1)
                pool.wait_ge(list_step, n + 4)
                pool.tensor_scalar(from_row[:, k], where[:, k], float(N - 1), None, ALU.min).then_inc(list_step, 1)
                pool.tensor_copy(to_row[:, k], where[:, k]).then_inc(list_step, 1)
                pool.wait_ge(list_step, n + 6)

            for done in xg_out:
                pool.wait_ge(done, 16 * QB)
            pool.wait_ge(wv_lo, 4)
            for k in range(NS):
                if k == 4:
                    split_values(0)
                    split_values(1)
                if k % (NS // 2) == 0:
                    slot_lists(k // (NS // 2))
                pool.indirect_dma_start(xg[:, k, :], None, xg_dram[:, :],
                                        bass.IndirectOffsetOnAxis(ap=from_row[:, k:k + 1], axis=0),
                                        bounds_check=N - 1, oob_is_err=True).then_inc(gathered[k // 4], 16)
            for i in range(E // 2):
                pool.wait_ge(gathered[i], 64)
                pool.sem_inc(pair_in, 1)
            pool.wait_ge(xb_out, 16 * (B + 1))
            for e in range(E):
                pool.wait_ge(hid_s, e + 1)
                pool.wait_ge(hid_hi, e + 1)
                pool.tensor_tensor(hidT[:, e % 2, LO, :], hid[:, e % 2, :], hidT[:, e % 2, HI, :],
                                   ALU.subtract).then_inc(hid_lo, 1)
                if e < 2 * QB and e % 2 == 1:
                    split_queries(B - QB + e // 2)
                if e < 2 * (VB - 1):
                    split_values(2 + e)
                if e == 1:
                    split_w_out(1)
                if e % 2 == 0:
                    continue
                for ee in (e - 1, e):
                    pool.wait_ge(y_s, ee + 1 + Y_CREDIT)
                    if ee > 0:
                        pool.wait_ge(added, 16 * CB * ee)
                    for j in range(CB):
                        k = ee * CB + j
                        pool.indirect_dma_start(sum_dram[:, :], bass.IndirectOffsetOnAxis(ap=to_row[:, k:k + 1], axis=0),
                                                y_sb[:, k, :], None, bounds_check=N + CAP - 1, oob_is_err=True,
                                                compute_op=ALU.add).then_inc(added, 16)
            pool.wait_ge(sum_in[0], 16)
            for it in range(ITS - 1):
                t = slice(it * STEPS, (it + 1) * STEPS)
                pool.wait_ge(o_done, (it + 1) * STEPS + O_CREDIT)
                pool.tensor_tensor(attn[:, t, :], attn[:, t, :], x_sb[:, t, :], ALU.add).then_inc(final, 1)

        @block.tensor
        def _(pe):
            def mm(o, a, b, first, last):
                return pe.matmul(o, a, b, start=first, stop=last)

            pe.wait_ge(consts_i, 8 + EB - 1)
            pe.wait_ge(small_lo, 3)
            pe.wait_ge(band_lo, 1)
            bank = psS[:, 0, 0, 0:3 * D].bitcast(F16)
            for s in (HI, LO):
                for w in range(3):
                    ins = pe.transpose(bank[:, (3 * s + w) * D:(3 * s + w + 1) * D], w_hl[:, s, w * D:(w + 1) * D], ident16[:])
            ins.then_inc(wT_ps, 1)
            def turn(b):
                for h in range(2):
                    g = 2 * b + h
                    pe.wait_ge(x_lo, g + 1)
                    pe.wait_ge(xT_s, g + 1 - 2 + XT_CREDIT)
                    bank = psT[:, h, :].bitcast(F16)
                    for s in (HI, LO):
                        for t in range(G):
                            ins = pe.transpose(bank[:, (s * G + t) * P:(s * G + t + 1) * P],
                                               xhl[:, g * G + t, s * D:(s + 1) * D],
                                               ident16[:])
                    ins.then_inc(xT_ps, 1)

            turn(0)
            pe.wait_ge(wT_s, 1)
            for c in range(2):
                o = psO[:, c * D:(c + 1) * D]
                (l_hi, r_hi), (l_lo, r_lo) = ((wT[:, s, 0:D], wT[:, s, D:2 * D]) if c == 0 else
                                              (wT[:, s, 2 * D:3 * D], owT[:, s, :]) for s in (HI, LO))
                mm(o, l_hi, r_hi, True, False)
                mm(o, l_hi, r_lo, False, False)
                ins = mm(o, l_lo, r_hi, False, True)
            ins.then_inc(fused_ps, 1)
            for b in range(B):
                if b + 1 < B:
                    turn(b + 1)
                for h in range(2):
                    g = 2 * b + h
                    pe.wait_ge(xT_s, g + 1 + XT_CREDIT)
                    for t in range(G):
                        n = g * G + t
                        o = psM[:, n * E:(n + 1) * E] if n < NT // 2 else psO[:, (n - NT // 2) * E:(n - NT // 2 + 1) * E]
                        at = slice((g * G + t) * P, (g * G + t + 1) * P)
                        mm(o, xT[:, HI, at], rw[:, HI, :], True, False)
                        mm(o, xT[:, HI, at], rw[:, LO, :], False, False)
                        ins = mm(o, xT[:, LO, at], rw[:, HI, :], False, True)
                    ins.then_inc(scores_r, 1)
                for h in range(2):
                    g = 2 * b + h
                    pe.wait_ge(fused_s, 3)
                    if 0 < b <= B - QB:
                        pe.wait_ge(query_lo, g - 1)
                    elif b > 0:
                        pe.wait_ge(unit_hi, 2 * g - 3)
                    o = psS[:, h, 0, :]
                    at = slice(g * GC, (g + 1) * GC)
                    mm(o, fused[:, HI, 0:D], xT[:, HI, at], True, False)
                    mm(o, fused[:, LO, 0:D], xT[:, HI, at], False, False)
                    mm(o, fused_mid[:, 0:D], xT[:, LO, at], False, True).then_inc(unit_ps, 1)
                    if b > 0:
                        if b - 1 < B - VB:
                            pe.wait_ge(value_lo, g - 1)
                        else:
                            pe.wait_ge(unit_hi, 2 * g - 2)
                    for t in range(G):
                        o = psS[:, h, 1, t * D:(t + 1) * D]
                        at = slice((g * G + t) * P, (g * G + t + 1) * P)
                        mm(o, xT[:, HI, at], fused[:, HI, D:2 * D], True, False)
                        mm(o, xT[:, HI, at], fused[:, LO, D:2 * D], False, False)
                        ins = mm(o, xT[:, LO, at], fused_mid[:, D:2 * D], False, True)
                    ins.then_inc(unit_ps, 1)

            def scores(i, batch, par):
                for c in range(2):
                    o = psS[:, par % 2, c, :]
                    at = bass.ds(i * P, P)
                    key = bass.ds(batch * T + c * 512, 512)
                    mm(o, qT[:, HI, at], kT[:, HI, key], True, False)
                    mm(o, qT[:, HI, at], kT[:, LO, key], False, False)
                    ins = mm(o, qT[:, LO, at], kT[:, HI, key], False, True)
                ins.then_inc(s_ready, 1)

            def turn_probs(i, par, first):
                pe.wait_ge(exp_done, i + 1)
                for h in range(2):
                    if not first:
                        pe.wait_ge(lo_done, 2 * (i - 1) + h + 1)
                    for k in range(4):
                        ins = pe.transpose(psT[:, h, k * P:(k + 1) * P], probs[:, par % 2, (4 * h + k) * P:(4 * h + k + 1) * P],
                                           ident[:])
                    ins.then_inc(pt_ready, 1)

            def weigh_values(i, batch, par):
                pe.wait_ge(lo_done, 2 * i + 2)
                pe.wait_ge(o_done, i + O_CREDIT)
                for k in range(BT):
                    ph, pl = (pT[:, par % 2, s, k * P:(k + 1) * P] for s in (HI, LO))
                    v_hi, v_lo = (vp[:, bass.ds(batch * BT + k, 1), s, :].rearrange("p a d -> p (a d)") for s in (HI, LO))
                    mm(psO[:, 0:D], ph, v_hi, k == 0, False)
                    mm(psO[:, 0:D], ph, v_lo, False, False)
                    ins = mm(psO[:, 0:D], pl, v_hi, False, k == BT - 1)
                ins.then_inc(pv_done, 1)

            def slot_rows(it, s, j):
                pe.wait_ge(plan_s, 1)
                pe.wait_ge(row_counts, 1)
                pe.wait_ge(own_s, 1)
                pe.wait_ge(row_sb, 2 * (EB * it + s) + j + ROW_CREDIT)
                h = bass.ds(it, 1)
                a = own[:, s, h, j * P:(j + 1) * P].rearrange("p a c -> p (a c)")
                mm(psM[:, 0:RC], a, row_src[:, h, :].rearrange("p a c -> p (a c)"), True, False)
                mm(psM[:, P:2 * P], a, row_lo[:, h, :].rearrange("p a c -> p (a c)"), False, True).then_inc(row_ps, 1)

            def turn_rows(p):
                pe.wait_ge(pair_in, p + 1)
                pe.wait_ge(y_s, 2 * p + Y_CREDIT)
                bank = psM[:].bitcast(F16)
                for q in range(2):
                    for s in (HI, LO):
                        for j in range(CB):
                            o = ((q * 2 + s) * CB + j) * P
                            ins = pe.transpose(bank[:, o:o + P], xg[:, bass.ds(4 * p + 2 * q + j, 1), s * D:(s + 1) * D]
                                               .rearrange("p a d -> p (a d)"), ident16[:])
                ins.then_inc(tt_ps, 1)

            def branch(e, q, off):
                for c in range(HB):
                    o = psM[:, c * CAP:(c + 1) * CAP]
                    wh, wl = (wv[:, s, bass.ds(e, 1), off + c * P:off + (c + 1) * P].rearrange("p a h -> p (a h)")
                              for s in (HI, LO))
                    mm(o, wh, xgT[:, q, HI, :], True, False)
                    mm(o, wl, xgT[:, q, HI, :], False, False)
                    ins = mm(o, wh, xgT[:, q, LO, :], False, True)
                return ins

            def expert_out(e, q):
                pe.wait_ge(hid_lo, e + 1)
                for j in range(CB):
                    o = psM[:, j * D:(j + 1) * D]
                    for c in range(HB):
                        hh, hl = (hidT[:, q, s, c * CAP + j * P:c * CAP + (j + 1) * P] for s in (HI, LO))
                        w_hi, w_lo = (wo[:, s, bass.ds(e, 1), c * D:(c + 1) * D].rearrange("p a d -> p (a d)")
                                      for s in (HI, LO))
                        mm(o, hh, w_hi, c == 0, False)
                        mm(o, hh, w_lo, False, False)
                        ins = mm(o, hl, w_hi, False, c == HB - 1)
                ins.then_inc(y_ps, 1)

            def steps(it, lists=False, experts=False, last=False, queries=None, w_out=None):
                for s in range(STEPS):
                    i = it * STEPS + s
                    e0 = 2 * (it - 2)
                    if queries is not None and s == 2:
                        pe.wait_ge(split_q, queries)
                    if not last or s < STEPS - 2:
                        pe.wait_ge(exp_done, i + 1)
                        scores(i + 2, (it + s // 2) >> 1, s + 2)
                    if lists:
                        slot_rows(it, s, 0)
                    if experts and s in (1, 2):
                        pe.wait_ge(xgT_s, it - 2 + 1)
                        if s == 2:
                            pe.wait_ge(hid_s, e0 + 1)
                        branch(e0 + s - 1, s - 1, H).then_inc(b_ps, 1)
                    if w_out is not None and s == 3:
                        pe.wait_ge(wo_lo, w_out)
                    if experts and s == 3:
                        pe.wait_ge(hid_s, e0 + 2)
                        expert_out(e0, 0)
                    if not last or s < STEPS - 1:
                        turn_probs(i + 1, s + 1, False)
                    if lists:
                        slot_rows(it, s, 1)
                    weigh_values(i, it >> 1, s)
                    if experts and s == 0:
                        turn_rows(it - 2)
                    if experts and s in (1, 2):
                        pe.wait_ge(silu_s, e0 + s)
                        branch(e0 + s - 1, s - 1, 0).then_inc(a_ps, 1)
                    if experts and s == 3:
                        pe.wait_ge(y_s, e0 + 1 + Y_CREDIT)
                        expert_out(e0 + 1, 1)

            pe.wait_ge(k_s, 2)
            pe.wait_ge(query_lo, 2 * (B - QB))
            pe.wait_ge(value_lo, 2 * (B - VB))
            pe.wait_ge(unit_hi, 4 * B - 2)
            scores(0, 0, 0)
            pe.wait_ge(unit_hi, 4 * B)
            scores(1, 0, 1)
            def counts(h, alone):
                return mm(psM[:, h * P:(h + 1) * P], mask[:, h * EB:(h + 1) * EB, :].rearrange("p e n -> p (e n)"), upper[:],
                          True, alone)

            pe.wait_ge(plan_in, 2)
            for h in range(NB):
                ins = counts(h, True)
            ins.then_inc(counts_ps, 1)
            pe.wait_ge(tot_s, 1)
            for h in range(NB):
                counts(h, False)
                ins = mm(psM[:, h * P:(h + 1) * P], below[:], tot[:, h:h + 1].to_broadcast([P, P]), False, True)
            ins.then_inc(all_counts_ps, 1)
            turn_probs(0, 0, True)
            pe.wait_ge(gates_s, 1)
            for h in range(NB):
                ins = pe.transpose(psO[:, h * P:(h + 1) * P],
                                   gates[:, h * EB:(h + 1) * EB, :].rearrange("p e n -> p (e n)"), ident[:])
            ins.then_inc(gates_ps, 1)
            pe.wait_ge(k_s, 2 * B)
            with pe.Fori(0, 2) as it:
                steps(it, lists=True)
            pe.wait_ge(row_sb, NS + ROW_CREDIT)
            pe.wait_ge(wv_lo, 4)
            with pe.Fori(1, 3) as pair:
                pe.wait_ge(split_v, pair * 4)
                steps(2 * pair, experts=True, w_out=pair)
                steps(2 * pair + 1, experts=True, queries=pair * 4)
            pe.wait_ge(split_v, 4 * VB)
            steps(6)
            steps(7, last=True)


_INS = ["x", "w_qkv", "out_wT", "out_b", "router_wT", "router_b", "w_in", "v_in", "w_out"]


def kernel(L0_attn_x, L0_attn_weight_qkv, L0_attn_out_w, L0_attn_out_b, L0_ffn_router_w, L0_ffn_router_b,
           L0_ffn_W, L0_ffn_V, L0_ffn_W_out):
    import numpy as _np
    import concourse.bacc as _bacc
    from concourse import mybir as _mybir
    from concourse.bass_utils import run_bass_kernel_spmd as _run

    given = [L0_attn_x, L0_attn_weight_qkv, _np.asarray(L0_attn_out_w).T, L0_attn_out_b,
             _np.asarray(L0_ffn_router_w).T, L0_ffn_router_b, L0_ffn_W, L0_ffn_V, L0_ffn_W_out]
    nc = _bacc.Bacc("TRN2", target_bir_lowering=False, num_devices=1)
    arrays, args = {}, []
    for name, a in zip(_INS, given):
        a = _np.ascontiguousarray(a)
        arrays[f"in_{name}"] = a
        args.append(nc.dram_tensor(f"in_{name}", a.shape, _mybir.dt.from_np(a.dtype), kind="ExternalInput").ap())
    args.append(nc.dram_tensor("out", arrays["in_x"].shape, F32, kind="ExternalOutput").ap())
    block_kernel(nc, *args)
    r = _run(nc, [arrays], core_ids=[0])
    return r.results[0]["out"]
```
